# Optimizing a Trainium2 kernel written in Bass

```python
import numpy as np
import jax
import jax.numpy as jnp

def _softmax(x, axis=-1):
    return jax.nn.softmax(x, axis=axis)

def _gelu(x):
    return jax.nn.gelu(x, approximate=True)

def _silu(x):
    return jax.nn.silu(x)

def _sigmoid(x):
    return jax.nn.sigmoid(x)

def _layernorm(x, axis=-1, eps=1e-05):
    m = jnp.mean(x, axis=axis, keepdims=True)
    v = jnp.var(x, axis=axis, keepdims=True)
    return (x - m) / jnp.sqrt(v + eps)

def _scatter_add(tgt, idx, src, axis=0):
    return tgt.at[idx].add(src)

def _segment_sum(src, seg, n):
    return jax.ops.segment_sum(src, seg, n)
kernel_name = 'mk_macaron_d1_jaxref_r4_919872'

def setup_inputs(seed: int=0):
    np.random.seed(seed)
    _w = jnp.asarray

    def _L0_attn_setup():
        import jax, jax.numpy as jnp
        import numpy as np
        D_MODEL = 512
        N_HEADS = 16
        D_HEAD = D_MODEL // N_HEADS
        B, S = (2, 512)
        EPS = 1e-05

        def _mhsa(X, ln_g, ln_b, Wq, bq, Wk, bk, Wv, bv, Wo, bo):
            n_ctx = X.shape[-2]
            mu = jnp.mean(X, axis=-1, keepdims=True)
            var = jnp.mean(jnp.square(X - mu), axis=-1, keepdims=True)
            Xn = (X - mu) * jax.lax.rsqrt(var + EPS) * ln_g + ln_b

            def split_heads(t):
                return t.reshape(t.shape[:-1] + (N_HEADS, D_HEAD)).swapaxes(-2, -3)
            Q = split_heads(Xn @ Wq + bq)
            K = split_heads(Xn @ Wk + bk)
            V = split_heads(Xn @ Wv + bv)
            scores = jnp.einsum('bhqd,bhkd->bhqk', Q, K) / jnp.sqrt(jnp.float32(D_HEAD))
            causal = jnp.tril(jnp.ones((n_ctx, n_ctx), dtype=bool))
            scores = jnp.where(causal, scores, jnp.float32(-jnp.inf))
            A = jax.nn.softmax(scores, axis=-1)
            AV = jnp.einsum('bhqk,bhkd->bhqd', A, V)
            AV = AV.swapaxes(-2, -3).reshape(X.shape[:-1] + (D_MODEL,))
            return AV @ Wo + bo
        key = jax.random.key(seed)
        ks = jax.random.split(key, 10)
        sd = 1.0 / np.sqrt(D_MODEL)
        inp = {'X': jax.random.normal(ks[0], (B, S, D_MODEL), dtype=jnp.float32), 'ln_g': jnp.ones((D_MODEL,), jnp.float32), 'ln_b': jnp.zeros((D_MODEL,), jnp.float32), 'Wq': jax.random.uniform(ks[1], (D_MODEL, D_MODEL), jnp.float32, -sd, sd), 'bq': jax.random.uniform(ks[2], (D_MODEL,), jnp.float32, -sd, sd), 'Wk': jax.random.uniform(ks[3], (D_MODEL, D_MODEL), jnp.float32, -sd, sd), 'bk': jax.random.uniform(ks[4], (D_MODEL,), jnp.float32, -sd, sd), 'Wv': jax.random.uniform(ks[5], (D_MODEL, D_MODEL), jnp.float32, -sd, sd), 'bv': jax.random.uniform(ks[6], (D_MODEL,), jnp.float32, -sd, sd), 'Wo': jax.random.uniform(ks[7], (D_MODEL, D_MODEL), jnp.float32, -sd, sd), 'bo': jax.random.uniform(ks[8], (D_MODEL,), jnp.float32, -sd, sd)}
        return inp
    _L0_attn_in = _L0_attn_setup()

    def _L0_ffn_setup():
        import jax, jax.numpy as jnp
        import numpy as np
        _FP4_LUT = jnp.array([0.0, 0.5, 1.0, 1.5, 2.0, 3.0, 4.0, 6.0, -0.0, -0.5, -1.0, -1.5, -2.0, -3.0, -4.0, -6.0], dtype=jnp.float32)
        GROUP_SIZE = 128
        EPS = 1e-06

        def _dequant_fp4(packed_i32, scales_f16, group_size):
            out_f, in_p = packed_i32.shape
            w = packed_i32.astype(jnp.uint32)
            shifts = jnp.arange(8, dtype=jnp.uint32) * 4
            nib = w[:, :, None] >> shifts & jnp.uint32(15)
            vals = _FP4_LUT[nib.astype(jnp.int32)].reshape(out_f, in_p * 8)
            s = scales_f16.astype(jnp.float32).T
            s_full = jnp.repeat(s, group_size, axis=1)
            return vals * s_full
        key = jax.random.key(seed)
        k1, k2, k3, k4, k5 = jax.random.split(key, 5)
        B, S, H, I = (4, 512, 512, 1408)
        x = jax.random.normal(k1, (B, S, H), dtype=jnp.float32)
        gate_up_packed = jax.random.randint(k2, (2 * I, H // 8), 0, 2147483647, dtype=jnp.int32)
        gate_up_scales = jax.random.uniform(k3, (H // GROUP_SIZE, 2 * I), dtype=jnp.float32).astype(jnp.float16)
        down_packed = jax.random.randint(k4, (H, I // 8), 0, 2147483647, dtype=jnp.int32)
        down_scales = jax.random.uniform(k5, (I // GROUP_SIZE, H), dtype=jnp.float32).astype(jnp.float16)
        return {'x': x, 'gate_up_packed': gate_up_packed, 'gate_up_scales': gate_up_scales, 'down_packed': down_packed, 'down_scales': down_scales}
    _L0_ffn_in = _L0_ffn_setup()
    _d = {'L0_attn_X': _L0_attn_in['X'], 'L0_attn_ln_g': _L0_attn_in['ln_g'], 'L0_attn_ln_b': _L0_attn_in['ln_b'], 'L0_attn_Wq': _L0_attn_in['Wq'], 'L0_attn_bq': _L0_attn_in['bq'], 'L0_attn_Wk': _L0_attn_in['Wk'], 'L0_attn_bk': _L0_attn_in['bk'], 'L0_attn_Wv': _L0_attn_in['Wv'], 'L0_attn_bv': _L0_attn_in['bv'], 'L0_attn_Wo': _L0_attn_in['Wo'], 'L0_attn_bo': _L0_attn_in['bo'], 'L0_ffn_gate_up_packed': _L0_ffn_in['gate_up_packed'], 'L0_ffn_gate_up_scales': _L0_ffn_in['gate_up_scales'], 'L0_ffn_down_packed': _L0_ffn_in['down_packed'], 'L0_ffn_down_scales': _L0_ffn_in['down_scales']}
    _x0 = _d['L0_attn_X']
    _d['L0_attn_X'] = jax.random.normal(jax.random.fold_in(jax.random.key(seed), 1), (2, 2048, 512), dtype=_x0.dtype)
    del _x0
    return _d

def reference(L0_attn_X, L0_attn_ln_g, L0_attn_ln_b, L0_attn_Wq, L0_attn_bq, L0_attn_Wk, L0_attn_bk, L0_attn_Wv, L0_attn_bv, L0_attn_Wo, L0_attn_bo, L0_ffn_gate_up_packed, L0_ffn_gate_up_scales, L0_ffn_down_packed, L0_ffn_down_scales):

    def _L0_attn_ref(X, ln_g, ln_b, Wq, bq, Wk, bk, Wv, bv, Wo, bo):
        import jax, jax.numpy as jnp
        import numpy as np
        D_MODEL = 512
        N_HEADS = 16
        D_HEAD = D_MODEL // N_HEADS
        B, S = (2, 512)
        EPS = 1e-05

        def _mhsa(X, ln_g, ln_b, Wq, bq, Wk, bk, Wv, bv, Wo, bo):
            n_ctx = X.shape[-2]
            mu = jnp.mean(X, axis=-1, keepdims=True)
            var = jnp.mean(jnp.square(X - mu), axis=-1, keepdims=True)
            Xn = (X - mu) * jax.lax.rsqrt(var + EPS) * ln_g + ln_b

            def split_heads(t):
                return t.reshape(t.shape[:-1] + (N_HEADS, D_HEAD)).swapaxes(-2, -3)
            Q = split_heads(Xn @ Wq + bq)
            K = split_heads(Xn @ Wk + bk)
            V = split_heads(Xn @ Wv + bv)
            scores = jnp.einsum('bhqd,bhkd->bhqk', Q, K) / jnp.sqrt(jnp.float32(D_HEAD))
            causal = jnp.tril(jnp.ones((n_ctx, n_ctx), dtype=bool))
            scores = jnp.where(causal, scores, jnp.float32(-jnp.inf))
            A = jax.nn.softmax(scores, axis=-1)
            AV = jnp.einsum('bhqk,bhkd->bhqd', A, V)
            AV = AV.swapaxes(-2, -3).reshape(X.shape[:-1] + (D_MODEL,))
            return AV @ Wo + bo
        return _mhsa(X, ln_g, ln_b, Wq, bq, Wk, bk, Wv, bv, Wo, bo)

    def _L0_ffn_ref(x, gate_up_packed, gate_up_scales, down_packed, down_scales):
        import jax, jax.numpy as jnp
        import numpy as np
        _FP4_LUT = jnp.array([0.0, 0.5, 1.0, 1.5, 2.0, 3.0, 4.0, 6.0, -0.0, -0.5, -1.0, -1.5, -2.0, -3.0, -4.0, -6.0], dtype=jnp.float32)
        GROUP_SIZE = 128
        EPS = 1e-06

        def _dequant_fp4(packed_i32, scales_f16, group_size):
            out_f, in_p = packed_i32.shape
            w = packed_i32.astype(jnp.uint32)
            shifts = jnp.arange(8, dtype=jnp.uint32) * 4
            nib = w[:, :, None] >> shifts & jnp.uint32(15)
            vals = _FP4_LUT[nib.astype(jnp.int32)].reshape(out_f, in_p * 8)
            s = scales_f16.astype(jnp.float32).T
            s_full = jnp.repeat(s, group_size, axis=1)
            return vals * s_full
        I = gate_up_packed.shape[0] // 2
        w_gu = _dequant_fp4(gate_up_packed, gate_up_scales, GROUP_SIZE)
        w_down = _dequant_fp4(down_packed, down_scales, GROUP_SIZE)
        gate_up = jnp.einsum('bsh,oh->bso', x, w_gu)
        gate, up = (gate_up[..., :I], gate_up[..., I:])
        h = jax.nn.silu(gate) * up
        y = jnp.einsum('bsi,hi->bsh', h, w_down)
        rms = jnp.sqrt(jnp.mean(y * y, axis=-1, keepdims=True) + EPS)
        return y / rms
    x = L0_attn_X
    x = x + 0.5 * _L0_ffn_ref(_layernorm(x, axis=-1), L0_ffn_gate_up_packed, L0_ffn_gate_up_scales, L0_ffn_down_packed, L0_ffn_down_scales)
    x = x + _L0_attn_ref(_layernorm(x, axis=-1), L0_attn_ln_g, L0_attn_ln_b, L0_attn_Wq, L0_attn_bq, L0_attn_Wk, L0_attn_bk, L0_attn_Wv, L0_attn_bv, L0_attn_Wo, L0_attn_bo)
    x = x + 0.5 * _L0_ffn_ref(_layernorm(x, axis=-1), L0_ffn_gate_up_packed, L0_ffn_gate_up_scales, L0_ffn_down_packed, L0_ffn_down_scales)
    return x

_drawn_inputs = setup_inputs


def setup_inputs(seed=0):
    import zlib

    import numpy as np

    out = dict(_drawn_inputs(seed))
    spreads = {'L0_attn_ln_g': (1.0, 0.6), 'L0_attn_ln_b': (0.0, 0.291)}
    factors = {'L0_attn_Wq': 6.877,
     'L0_attn_bq': 8.0,
     'L0_attn_Wk': 6.891,
     'L0_attn_bk': 8.0,
     'L0_attn_bv': 4.349,
     'L0_attn_bo': 2.689}
    for name, (base, spread) in spreads.items():
        noise = np.random.default_rng([zlib.crc32(name.encode()), seed]).standard_normal(out[name].shape)
        drawn = base * np.exp(spread * noise) if base else spread * noise
        out[name] = jnp.asarray(drawn.astype(out[name].dtype))
    for name, factor in factors.items():
        out[name] = (out[name] * factor).astype(out[name].dtype)
    return out
```

```python
import concourse.bass as bass
import concourse.mybir as mybir

F32 = mybir.dt.float32
F32R = mybir.dt.float32r
F16 = mybir.dt.float16
BF16 = mybir.dt.bfloat16
I32 = mybir.dt.int32
U16 = mybir.dt.uint16
ALU = mybir.AluOpType
ACT = mybir.ActivationFunctionType
AX = mybir.AxisListType

B, S, D, H, DH = 2, 2048, 512, 16, 32
T = B * S
I = 1408
IC = I // 128
KC = D // 128
NT = T // 512
J = 128.0
SC = float(1.0 / (32.0 ** 0.5))
NEG = -1.0e30
BASE = 16512


class Lane:

    def __init__(self, nc, name):
        self.nc, self.name = nc, name
        self.items, self.seen = [], {}
        self.phase = 0
        self.fresh()

    def fresh(self):
        self.sem = self.nc.alloc_semaphore(f"{self.name}{self.phase}")
        self.key = f"{self.name}{self.phase}"
        self.phase += 1
        self.n = 0

    def need(self, *toks):
        for t in toks:
            if t is None:
                continue
            key, sem, value = t
            if self.seen.get(key, 0) >= value:
                continue
            self.seen[key] = value
            self.items.append(lambda e, sem=sem, value=value: e.wait_ge(sem, value))

    def do(self, fn, *toks, sig=True):
        self.need(*toks)
        if not sig:
            self.items.append(fn)
            return None
        self.n += 1
        sem = self.sem
        self.items.append(lambda e: fn(e).then_inc(sem, 1))
        return (self.key, sem, self.n)

    def last(self):
        return (self.key, self.sem, self.n) if self.n else None

    def run(self, e):
        for f in self.items:
            f(e)


class Dma:

    N = 32

    def __init__(self, nc, sp):
        self.sp = sp
        self.sems = [nc.alloc_semaphore(f"dma{i}") for i in range(self.N)]
        self.count = [0] * self.N
        self.i = 0

    def go(self, dst, src, *toks):
        k = self.i % self.N
        self.i += 1
        sem = self.sems[k]
        if self.count[k]:
            self.sp.need((f"dma{k}", sem, self.count[k]))
        self.count[k] += 16
        self.sp.need(*toks)
        self.sp.items.append(lambda e: e.dma_start(dst, src).then_inc(sem, 16))
        return (f"dma{k}", sem, self.count[k])

    def all(self):
        return [(f"dma{k}", self.sems[k], c) for k, c in enumerate(self.count) if c]


class Prog:
    def __init__(self, nc, a):
        self.nc, self.a = nc, a
        self.pe, self.dve, self.act = Lane(nc, "pe"), Lane(nc, "dve"), Lane(nc, "act")
        self.pool, self.sp = Lane(nc, "pool"), Lane(nc, "sp")
        self.lanes = [self.pe, self.dve, self.act, self.pool, self.sp]
        self.dma = Dma(nc, self.sp)
        self.nuid = 0

    def at(self, shape, dt, off):
        self.nuid += 1
        return self.nc.alloc_sbuf_tensor_at(f"sb{self.nuid}", list(shape), dt, offset=BASE + off)

    def barrier(self):
        toks = [ln.last() for ln in self.lanes] + self.dma.all()
        for ln in self.lanes:
            ln.need(*toks)
        for ln in self.lanes:
            ln.fresh()

    def mm(self, out, l, r, st, sp, *toks, sig=False):
        return self.pe.do(lambda e: e.matmul(out, l, r, start=st, stop=sp), *toks, sig=sig)

    def tr(self, out, x, ident, *toks, sig=False):
        return self.pe.do(lambda e: e.transpose(out, x, ident), *toks, sig=sig)

    def af(self, out, x, func, *toks, **kw):
        return self.act.do(lambda e: e.activation(out, x, func, **kw), *toks)

    def tt(self, ln, out, x, y, op, *toks):
        return ln.do(lambda e: e.tensor_tensor(out, x, y, op), *toks)

    def ts(self, ln, out, x, s1, s2, op0, op1, *toks):
        if op1 is None:
            return ln.do(lambda e: e.tensor_scalar(out, x, s1, None, op0), *toks)
        return ln.do(lambda e: e.tensor_scalar(out, x, s1, s2, op0, op1), *toks)

    def stt(self, out, x, s, y, op0, op1, *toks):
        return self.dve.do(lambda e: e.scalar_tensor_tensor(out, x, s, y, op0, op1), *toks)

    def cp(self, ln, out, x, *toks):
        return ln.do(lambda e: e.tensor_copy(out, x), *toks)

    def rsqrt(self, out, x, scale, eps, mult, w, *toks):
        v, g, t = w[:, 0, :], w[:, 1, :], w[:, 2, :]
        d = self.dve
        k = self.ts(d, v, x, scale, eps, ALU.mult, ALU.add, *toks)
        k = self.ts(d, t.bitcast(I32), v.bitcast(I32), 1, None, ALU.logical_shift_right, None, k)
        k = self.ts(d, g.bitcast(I32), t.bitcast(I32), -1.0, float(0x5F3759DF), ALU.mult, ALU.add, k)
        for n in range(4):
            k = self.tt(d, t, g, g, ALU.mult, k)
            k = self.tt(d, t, t, v, ALU.mult, k)
            k = self.ts(d, t, t, -0.5, 1.5, ALU.mult, ALU.add, k)
            k = self.tt(d, out if n == 3 and mult == 1.0 else g, g, t, ALU.mult, k)
        if mult != 1.0:
            k = self.ts(d, out, g, mult, None, ALU.mult, None, k)
        return k


def constants(p):
    o = 0

    def take(shape, dt, size):
        nonlocal o
        t = p.at(shape, dt, o)
        o += (size + 31) // 32 * 32
        return t

    p.idf = take([128, 128], F32, 512)
    p.idh = take([128, 128], F16, 256)
    p.idb = take([128, 128], BF16, 256)
    p.mS = take([128, 128], BF16, 256)
    p.mT = take([128, 128], BF16, 256)
    p.ones = take([128, 32], F32, 128)
    p.st = take([128, 4, 6], F32, 96)
    p.mv = take([128, 4, 2], F32, 32)
    p.rs = take([128, 4], F32, 32)
    p.w4 = take([128, 3, 4], F32, 48)
    p.ss = take([128, 4], F32, 32)
    p.r4 = take([128, 4], F32, 32)
    p.w5 = take([128, 3, 4], F32, 48)
    p.st2 = take([128, 4, 6], F32, 96)
    p.mv2 = take([128, 4, 2], F32, 32)
    p.rs2 = take([128, 4], F32, 32)
    p.bias = take([128, 4, 4], F32, 64)
    p.bvb = take([128, 512], F32, 2048)
    p.bob = take([128, 512], F32, 2048)
    p.sg = take([128, 22, 4], F32, 352)
    p.sd = take([128, 4, 11], F32, 176)
    assert o <= 8192
    a, pool = p.a, p.pool
    k0 = pool.do(lambda e: e.memset(p.idf[:, :], 0.0))
    k1 = pool.do(lambda e: e.memset(p.mS[:, :], 0.0))
    k2 = pool.do(lambda e: e.memset(p.mT[:, :], 0.0))
    pool.do(lambda e: e.memset(p.ones[:, :], 1.0))
    k0 = pool.do(lambda e: e.affine_select(out=p.idf[:, :], in_=p.idf[:, :], compare_op=ALU.not_equal, fill=1.0,
                                           base=0, pattern=[[-1, 128]], channel_multiplier=1), k0)
    pool.do(lambda e: e.affine_select(out=p.mS[:, :], in_=p.mS[:, :], compare_op=ALU.is_ge, fill=NEG,
                                      base=0, pattern=[[-1, 128]], channel_multiplier=1), k1)
    pool.do(lambda e: e.affine_select(out=p.mT[:, :], in_=p.mT[:, :], compare_op=ALU.is_ge, fill=NEG,
                                      base=0, pattern=[[1, 128]], channel_multiplier=-1), k2)
    p.cp(pool, p.idh[:, :], p.idf[:, :], k0)
    p.cp(pool, p.idb[:, :], p.idf[:, :], k0)
    rows = p.at([16, 128], F32, 143360)
    ks = [p.dma.go(rows[4 * n:4 * n + 4, :], a[f"L0_attn_{name}"].rearrange("(c p) -> c p", p=128))
          for n, name in enumerate(("ln_g", "ln_b", "bq", "bk"))]
    k = p.tr(p.b[7][:, 0:16], rows[:, :], p.idf[0:16, 0:16], k0, *ks, sig=True)
    k = p.cp(p.dve, p.bias[:, :, :].rearrange("p a b -> p (a b)"), p.b[7][:, 0:16], k)
    p.ts(p.dve, p.bias[:, 2, :], p.bias[:, 2, :], SC, None, ALU.mult, None, k)
    p.barrier()
    p.dma.go(p.bvb[:, :], a["L0_attn_bv"].partition_broadcast(128))
    p.dma.go(p.bob[:, :], a["L0_attn_bo"].partition_broadcast(128))


def psum(p):
    p.bank = [p.nc.alloc_psum_tensor(f"ps{i}", [128, 512], F32) for i in range(2)]
    p.pair = [p.nc.alloc_psum_tensor(f"pp{i}", [128, 2, 512], F32) for i in range(3)]
    p.b = [p.bank[0][:, :], p.bank[1][:, :]] + [p.pair[i][:, n, :] for i in range(3) for n in range(2)]


def ffn_memory(p):
    o = 8192
    p.wga, p.wgb = p.at([128, KC, 2 * I], F32R, o), p.at([128, KC, 2 * I], F32R, o + 45056)
    p.wda, p.wdb = p.at([128, IC, D], F32R, o + 90112), p.at([128, IC, D], F32R, o + 112640)
    o = 143360
    p.x1 = [p.at([128, KC, 512], F32R, o + 8192 * i) for i in range(2)]
    p.x2 = [p.at([128, KC, 512], F32R, o + 16384 + 8192 * i) for i in range(2)]
    o = 176128
    p.h1 = [p.at([128, 512], F32R, o + 2048 * i) for i in range(3)]
    p.h2 = [p.at([128, 512], F32R, o + 6144 + 2048 * i) for i in range(3)]
    p.sil = [p.at([128, 512], F32, o + 12288 + 2048 * i) for i in range(2)]
    p.h = [p.at([128, 512], F32, o + 16384 + 2048 * i) for i in range(2)]
    o = 196608
    p.xb = [p.at([128, 512], F32, o + 2048 * i) for i in range(4)]
    p.xr = [p.at([128, 512], F32, o + 8192 + 2048 * i) for i in range(3)]
    p.junk = p.at([128, 512], BF16, o + 14336)


def dequant(p):
    o = 143360
    pk = p.at([128, 22, 64], I32, o)
    pd = p.at([128, 4, 176], I32, o + 5632)
    v16 = p.at([128, 2816, 4], U16, o + 8448)
    v16d = p.at([128, 1408, 4], U16, o + 30976)
    t1 = [p.at([128, 1408], U16, o + 42240 + 2816 * i) for i in range(2)]
    w32 = [p.at([128, 4, 128], F32, o + 47872 + 2048 * i) for i in range(3)]
    w32d = [p.at([128, 11, 128], F32, o + 54016 + 5632 * i) for i in range(2)]
    sc16 = p.at([11, 2816 + 512], F16, 98304 + 13312)
    sc32 = p.at([11, 2816 + 512], F32, 98304)
    a, dve = p.a, p.dve
    kpk = p.dma.go(pk[:, :, :], a["L0_ffn_gate_up_packed"].rearrange("(t p) w -> p t w", p=128))
    ks1 = p.dma.go(sc16[0:4, 0:2816], a["L0_ffn_gate_up_scales"])
    ks2 = p.dma.go(sc16[0:11, 2816:3328], a["L0_ffn_down_scales"])
    kpd = p.dma.go(pd[:, :, :], a["L0_ffn_down_packed"].rearrange("(t p) w -> p t w", p=128))
    c1 = p.af(sc32[0:4, 0:2816], sc16[0:4, 0:2816], ACT.Copy, ks1, scale=16384.0)
    c2 = p.af(sc32[0:11, 2816:3328], sc16[0:11, 2816:3328], ACT.Copy, ks2, scale=16384.0)
    p.pe.need(p.pool.last())
    for t in range(22):
        k1 = p.tr(p.b[0][:, 4 * t:4 * t + 4], sc32[0:4, 128 * t:128 * t + 128], p.idf[0:4, 0:4], c1, sig=t == 21)
    for t in range(4):
        k2 = p.tr(p.b[1][:, 11 * t:11 * t + 11], sc32[0:11, 2816 + 128 * t:2944 + 128 * t], p.idf[0:11, 0:11], c2,
                  sig=t == 3)
    e1 = p.af(p.sg[:, :, :].rearrange("p a b -> p (a b)"), p.b[0][:, 0:88], ACT.Copy, k1)
    e2 = p.af(p.sd[:, :, :].rearrange("p a b -> p (a b)"), p.b[1][:, 0:44], ACT.Copy, k2)

    tfree = [None, None]

    def decode(src, dst, n0, n1, *toks):
        u = src[:, n0:n1]
        pend = []
        last = []
        for i in range(5):
            if i < 4:
                t = t1[i % 2][:, 0:n1 - n0]
                ka = p.ts(dve, t, u, 12 - 4 * i, 0x8000, ALU.logical_shift_left, ALU.bitwise_and, tfree[i % 2], *toks)
                sh = 9 - 4 * i
                op = ALU.logical_shift_left if sh >= 0 else ALU.logical_shift_right
                kb = p.ts(dve, dst[:, n0:n1, i], u, abs(sh), 0x0E00, op, ALU.bitwise_and)
                pend.append((i, t, kb))
            if i >= 1:
                m, t, kb = pend.pop(0)
                tfree[m % 2] = p.tt(dve, dst[:, n0:n1, m], dst[:, n0:n1, m], t, ALU.bitwise_or, kb)
                last.append(tfree[m % 2])
        return last[-1]

    ug = pk[:, :, :].rearrange("p a b -> p (a b)").bitcast(U16)
    ud = pd[:, :, :].rearrange("p a b -> p (a b)").bitcast(U16)
    vg = v16[:, :, :].rearrange("p a b -> p (a b)").bitcast(F16)
    vd = v16d[:, :, :].rearrange("p a b -> p (a b)").bitcast(F16)
    free = [e1, e2, None, None]
    wfree = [None] * 3
    n = 0

    def split(bank, outa, outb, k):
        ka = p.af(outa, bank, ACT.Copy, k)
        return p.stt(outb, outa, -127.0 / 128.0, bank, ALU.mult, ALU.add, ka)

    for half in range(2):
        kd = decode(ug, v16, 1408 * half, 1408 * half + 1408, kpk)
        for t in range(11 * half, 11 * half + 11):
            w = w32[t % 3]
            kw = p.tt(dve, w[:, :, :], vg[:, 512 * t:512 * t + 512].rearrange("p (g i) -> p g i", g=4),
                      p.sg[:, t, :].unsqueeze(2).broadcast_to([128, 4, 128]), ALU.mult, kd, e1, wfree[t % 3])
            bk = p.b[n % 4]
            for g in range(4):
                k = p.tr(bk[:, 128 * g:128 * g + 128], w[:, g, :], p.idf[:, :], kw, free[n % 4], sig=g == 3)
            wfree[t % 3] = k
            free[n % 4] = split(bk.rearrange("p (g i) -> p g i", g=4), p.wga[:, :, 128 * t:128 * t + 128],
                                p.wgb[:, :, 128 * t:128 * t + 128], k)
            n += 1
    kd = decode(ud, v16d, 0, 1408, kpd)
    wfree = [None] * 2
    for t in range(4):
        w = w32d[t % 2]
        kw = p.tt(dve, w[:, :, :], vd[:, 1408 * t:1408 * t + 1408].rearrange("p (g i) -> p g i", g=11),
                  p.sd[:, t, :].unsqueeze(2).broadcast_to([128, 11, 128]), ALU.mult, kd, e2, wfree[t % 2])
        for g0 in range(0, 11, 4):
            m = min(4, 11 - g0)
            bk = p.b[n % 4]
            for g in range(m):
                k = p.tr(bk[:, 128 * g:128 * g + 128], w[:, g0 + g, :], p.idf[:, :], kw, free[n % 4], sig=g == m - 1)
            free[n % 4] = split(bk[:, 0:128 * m].rearrange("p (g i) -> p g i", g=m),
                                p.wda[:, g0:g0 + m, 128 * t:128 * t + 128], p.wdb[:, g0:g0 + m, 128 * t:128 * t + 128], k)
            n += 1
        wfree[t % 2] = k


def spill_views(p):
    out = []
    for w, d, n in ((p.wga, p.dga, 11264), (p.wgb, p.dgb, 11264), (p.wda, p.dda, 5632), (p.wdb, p.ddb, 5632)):
        v = w[:, :, :].rearrange("p a b -> p (a b)").bitcast(F32)
        out.append([(v[:, n // 8 * i:n // 8 * (i + 1)], d[:, n // 8 * i:n // 8 * (i + 1)]) for i in range(8)])
    return out


def ffn(p, src, dst, spill):
    pe, dve, act, pool = p.pe, p.dve, p.act, p.pool
    TB = p.b[0]
    ring = [p.b[1], p.b[2], p.b[3]]
    Y = p.b[4:8]
    srcv = src.rearrange("(n t p) d -> n t p d", t=4, p=128)
    dstv = dst.rearrange("(n t p) d -> n t p d", t=4, p=128)
    tb_free = [None]
    xb_free = [None] * 4
    mv_free = [None]
    x_free = [None, None]
    x_ready = {}

    def stats(tt):
        ks = []
        for tb in range(4):
            kl = p.dma.go(p.xb[tb][:, :], srcv[tt, tb], xb_free[tb])
            o, x = p.st[:, tb, :], p.xb[tb][:, :]
            k = dve.do(lambda e, o=o, x=x: e.bn_stats(o, x), kl)
            m = p.mv[:, tb, :]
            k = dve.do(lambda e, o=o, m=m: e.bn_aggr(m, o), k, mv_free[0])
            ks.append(k)
        k = p.rsqrt(p.rs[:, :], p.mv[:, :, 1], 1.0, 1e-5, 128.0, p.w4, *ks)
        out = []
        for tb in range(4):
            out.append(p.ts(pool, p.xb[tb][:, :], p.xb[tb][:, :], p.mv[:, tb, 0:1], p.rs[:, tb:tb + 1],
                            ALU.subtract, ALU.mult, k))
        mv_free[0] = out[3]
        return out

    def chunk(tt, c, kn):
        for tb in range(4):
            k = p.tr(TB[:, 128 * tb:128 * tb + 128], p.xb[tb][:, 128 * c:128 * c + 128], p.idf[:, :], kn[tb],
                     tb_free[0], sig=tb == 3)
            if c == 3:
                xb_free[tb] = k
        if c == 3:
            for tb in range(4):
                xb_free[tb] = k
        i = tt % 2
        ka = p.af(p.x1[i][:, c, :], TB, ACT.Copy, k, x_free[i], scale=(1.0 - 1.0 / J) / J)
        kb = p.stt(p.x2[i][:, c, :], p.x1[i][:, c, :], -J, TB, ALU.mult, ALU.add, ka)
        tb_free[0] = kb
        x_ready[tt] = kb

    ring_free = [None] * 3
    nring = [0]
    sil_free, h_free = [None] * 2, [None] * 2
    hh_free = [None] * 3
    h_ready = {}
    y_free = [None] * 4

    def proj(tt, col):
        r = nring[0] % 3
        nring[0] += 1
        i = tt % 2
        for c in range(KC):
            p.mm(ring[r], p.wga[:, c, col:col + 128], p.x1[i][:, c, :], c == 0, False, ring_free[r], x_ready[tt])
            k = p.mm(ring[r], p.wgb[:, c, col:col + 128], p.x2[i][:, c, :], False, c == KC - 1, sig=c == KC - 1)
        return r, k

    def up(tt, i):
        u = tt * IC + i
        rg, kg = proj(tt, 128 * i)
        s, h = p.sil[u % 2], p.h[u % 2]
        h1, h2 = p.h1[u % 3], p.h2[u % 3]
        ks = p.af(s[:, :], ring[rg], ACT.Silu, kg, sil_free[u % 2])
        ring_free[rg] = ks
        ru, ku = proj(tt, I + 128 * i)
        if i == IC - 1:
            x_free[tt % 2] = ku
        kh = p.stt(h[:, :], s[:, :], J, ring[ru], ALU.mult, ALU.mult, ks, ku, h_free[u % 2])
        ring_free[ru] = kh
        sil_free[u % 2] = kh
        k1 = p.af(h1[:, :], h[:, :], ACT.Copy, kh, hh_free[u % 3], scale=(1.0 - 1.0 / J) / J)
        k2 = p.stt(h2[:, :], h1[:, :], -J, h[:, :], ALU.mult, ALU.add, k1)
        h_free[u % 2] = k2
        h_ready[u] = k2

    def down(tt, i):
        u = tt * IC + i
        h1, h2 = p.h1[u % 3], p.h2[u % 3]
        for tb in range(4):
            c = slice(128 * tb, 128 * tb + 128)
            p.mm(Y[tb], h1[:, c], p.wda[:, i, :], i == 0, False, h_ready[u], y_free[tb])
            k = p.mm(Y[tb], h2[:, c], p.wdb[:, i, :], False, i == IC - 1, sig=i == IC - 1 or tb == 3)
            if i == IC - 1:
                ky[tb] = k
        hh_free[u % 3] = k

    ky = [None] * 4
    xr_free = [None] * 3
    nxr = [0]
    r4_free = [None]

    def finish(tt):
        kl, slot = [], []
        ks = []
        for tb in range(4):
            o = p.ss[:, tb:tb + 1]
            ks.append(p.af(p.junk[:, :], Y[tb], ACT.Square, ky[tb], r4_free[0], act.last(), accum_out=o))
        k = p.rsqrt(p.r4[:, :], p.ss[:, :], 1.0 / D, 1e-6, 0.5, p.w5, *ks)
        for tb in range(4):
            s = nxr[0] % 3
            nxr[0] += 1
            kx = p.dma.go(p.xr[s][:, :], srcv[tt, tb], xr_free[s])
            ko = p.stt(p.xr[s][:, :], Y[tb], p.r4[:, tb:tb + 1], p.xr[s][:, :], ALU.mult, ALU.add, kx, k)
            y_free[tb] = ko
            xr_free[s] = p.dma.go(dstv[tt, tb], p.xr[s][:, :], ko)
        r4_free[0] = ko

    kn = stats(0)
    for c in range(KC):
        chunk(0, c, kn)
    units = [(tt, i) for tt in range(NT) for i in range(IC)]
    for tt, i in units:
        if i == 1 and tt + 1 < NT:
            kn = stats(tt + 1)
        up(tt, i)
        if i in (3, 5, 7, 9) and tt + 1 < NT:
            chunk(tt + 1, (i - 3) // 2, kn)
        if i == 0 and tt:
            down(tt - 1, IC - 1)
            finish(tt - 1)
        elif i == 2:
            down(tt, 0)
            down(tt, 1)
        elif i > 2:
            down(tt, i - 1)
        if spill is not None and i == 5:
            for w in spill:
                s, d = w[tt]
                p.dma.go(d, s)
    down(NT - 1, IC - 1)
    finish(NT - 1)


def qkv(p, b):
    pe, dve, act, pool = p.pe, p.dve, p.act, p.pool
    a = p.a
    o = 106496
    wh = [p.at([128, KC, D], F32R, o + 16384 * i) for i in range(3)]
    wl = [p.at([128, KC, D], F32R, o + 16384 * i + 8192) for i in range(3)]
    o += 49152
    xb = [p.at([128, 512], F32, o + 2048 * i) for i in range(4)]
    xnt = [p.at([128, 512], F32, o + 8192 + 2048 * i) for i in range(2)]
    q32 = [p.at([128, 512], F32, o + 12288 + 2048 * i) for i in range(2)]
    o += 16384
    xh = [p.at([128, KC, 512], F32R, o + 16384 * i) for i in range(2)]
    xl = [p.at([128, KC, 512], F32R, o + 16384 * i + 8192) for i in range(2)]
    wraw = [p.at([128, KC, D], F32, o + 16384 + 8192 * i) for i in range(2)]
    wfree = [None, None]
    kw = []
    for n, name in enumerate(("Wq", "Wk", "Wv")):
        w = wraw[n % 2]
        k = p.dma.go(w[:, :, :], a[f"L0_attn_{name}"].rearrange("(c p) n -> p c n", p=128), wfree[n % 2])
        k = p.cp(dve, wh[n][:, :, :], w[:, :, :], k)
        k = p.tt(dve, wl[n][:, :, :], w[:, :, :], wh[n][:, :, :], ALU.subtract, k)
        wfree[n % 2] = k
        kw.append(k)
    srcv = p.xa[S * b:S * (b + 1), :].rearrange("(n t p) d -> n t p d", t=4, p=128)
    tbank = [p.b[0], p.b[1]]
    t_free = [None, None]
    ring = p.b[2:8]
    ring_free = [None] * 6
    nr = [0]
    xb_free = [None] * 4
    xnt_free, q32_free, x_free = [None] * 2, [None] * 2, [wfree[0], wfree[1]]
    x_free = [None, kw[2]]
    s_free = [None, None]
    x_ready = {}
    nx, nq = [0], [0]

    def norm(tt):
        for rnd in range(2):
            st, mv, rs = (p.st, p.mv, p.rs) if rnd == 0 else (p.st2, p.mv2, p.rs2)
            ks = []
            for tb in range(4):
                if rnd == 0:
                    kl = p.dma.go(xb[tb][:, :], srcv[tt, tb], xb_free[tb])
                else:
                    kl = kn[tb]
                o_, x_, m_ = st[:, tb, :], xb[tb][:, :], mv[:, tb, :]
                k = dve.do(lambda e, o=o_, x=x_: e.bn_stats(o, x), kl)
                ks.append(dve.do(lambda e, o=o_, m=m_: e.bn_aggr(m, o), k, s_free[rnd]))
            k = p.rsqrt(rs[:, :], mv[:, :, 1], 1.0, 1e-5, 1.0, p.w4 if rnd == 0 else p.w5, *ks)
            kn = []
            for tb in range(4):
                kn.append(p.ts(pool, xb[tb][:, :], xb[tb][:, :], mv[:, tb, 0:1], rs[:, tb:tb + 1],
                               ALU.subtract, ALU.mult, k))
            s_free[rnd] = kn[3]
        i = tt % 2
        for c in range(KC):
            f = c % 2
            for tb in range(4):
                k = p.tr(tbank[f][:, 128 * tb:128 * tb + 128], xb[tb][:, 128 * c:128 * c + 128], p.idf[:, :], kn[tb],
                         t_free[f], sig=tb == 3)
            s = nx[0] % 2
            nx[0] += 1
            ka = p.af(xnt[s][:, :], tbank[f], ACT.Identity, k, xnt_free[s], scale=p.bias[:, 0, c:c + 1],
                      bias=p.bias[:, 1, c:c + 1])
            t_free[f] = ka
            kh = p.cp(dve, xh[i][:, c, :], xnt[s][:, :], ka, x_free[i])
            kl = p.tt(dve, xl[i][:, c, :], xnt[s][:, :], xh[i][:, c, :], ALU.subtract, kh)
            xnt_free[s] = kl
        for tb in range(4):
            xb_free[tb] = k
        x_ready[tt] = kl

    def group(tt, lh, ll, rh, rl, kw):
        r = nr[0] % 6
        nr[0] += 1
        for c in range(KC):
            p.mm(ring[r], lh(c), rh(c), c == 0, False, ring_free[r], x_ready[tt], kw)
            p.mm(ring[r], lh(c), rl(c), False, False)
            k = p.mm(ring[r], ll(c), rh(c), False, c == KC - 1, sig=c == KC - 1)
        return r, k

    def proj(tt):
        i = tt % 2
        ts_ = slice(512 * tt, 512 * tt + 512)
        for f in range(4):
            fs = slice(128 * f, 128 * f + 128)
            for n, dst in ((0, p.qs), (1, p.ks)):
                r, k = group(tt, lambda c: wh[n][:, c, fs], lambda c: wl[n][:, c, fs], lambda c: xh[i][:, c, :],
                             lambda c: xl[i][:, c, :], kw[n])
                s = nq[0] % 2
                nq[0] += 1
                ka = p.af(q32[s][:, :], ring[r], ACT.Identity, k, q32_free[s], scale=SC if n == 0 else 1.0,
                          bias=p.bias[:, 2 + n, f:f + 1])
                ring_free[r] = ka
                kh = p.cp(dve, dst[:, f, 0, ts_], q32[s][:, :], ka)
                q32_free[s] = p.tt(pool, dst[:, f, 1, ts_], q32[s][:, :], dst[:, f, 0, ts_], ALU.subtract, kh)
        for tb in range(4):
            c0 = slice(128 * tb, 128 * tb + 128)
            r, k = group(tt, lambda c: xh[i][:, c, c0], lambda c: xl[i][:, c, c0], lambda c: wh[2][:, c, :],
                         lambda c: wl[2][:, c, :], kw[2])
            ring_free[r] = p.tt(dve, p.v[:, 4 * tt + tb, :], ring[r], p.bvb[:, :], ALU.add, k)
        x_free[i] = k

    norm(0)
    for tt in range(4):
        if tt < 3:
            norm(tt + 1)
        proj(tt)


def attention(p, b):
    pe, dve, act, pool = p.pe, p.dve, p.act, p.pool
    o = 106496
    kp = [p.at([128, 4, S], F16, o + 16384 * i) for i in range(2)]
    qp = [p.at([128, 4, S], F16, o + 32768 + 16384 * i) for i in range(2)]
    o += 65536
    E = [p.at([128, 4, 512], F32, o + 8192 * i) for i in range(2)]
    o += 16384
    rec = p.at([128, 512], F32, o)
    pm = [p.at([128, 16, 4], F32, o + 2048 + 256 * i) for i in range(2)]
    nm = [p.at([128, 4, 4], F32, o + 2560 + 64 * i) for i in range(2)]
    mc = [p.at([128, 4, 32], F16, o + 2688 + 256 * i) for i in range(2)]
    mbank = [p.b[0], p.b[1]]
    st = [p.pair[0], p.pair[1]]
    AV, RS = p.b[6], p.b[7]
    avn = p.qs[:, :, :, :].rearrange("p g a s -> p g (a s)").bitcast(F32)

    kc = []
    for i in range(2):
        k = pool.do(lambda e, x=kp[i]: e.memset(x[96:128, :, :], 0.0))
        for s in range(2):
            k = pool.do(lambda e, x=kp[i], s=s: e.affine_select(
                out=x[96:128, :, :], in_=x[96:128, :, :], compare_op=ALU.not_equal, fill=1.0, base=-4 * s,
                pattern=[[-1, 4], [0, S]], channel_multiplier=1), k)
        kc.append(k)
    km = [pool.do(lambda e, x=mc[i]: e.memset(x[:, :, :], 0.0), kc[1]) for i in range(2)]
    pool.need(km[1])
    mc_free = [km[0], km[1]]

    last_use = {}
    stacked = {}

    def restack(hg):
        i = hg % 2
        ks = []
        for j in range(4):
            rows = slice(32 * j, 32 * j + 32)
            for r, w in ((0, 0), (1, 1), (2, 0)):
                ks.append(p.dma.go(kp[i][32 * r:32 * r + 32, j, :], p.ks[rows, hg, w, :], last_use.get(hg - 2)))
            for r, w in ((0, 0), (1, 0), (2, 1)):
                ks.append(p.dma.go(qp[i][32 * r:32 * r + 32, j, :], p.qs[rows, hg, w, :], last_use.get(hg - 2)))
        stacked[hg] = ks

    m_free = [None, None]
    nmx = [0]
    pm_free, nm_free = [None, None], [None, None]
    ngrp = [0]
    biased = {}

    def max_units():
        pend = None
        for hg in range(4):
            i = hg % 2
            for qt in range(4):
                g = ngrp[0] % 2
                ngrp[0] += 1
                cnt = 0
                for qb in range(4):
                    q0 = 512 * qt + 128 * qb
                    nk = q0 + 128
                    for j in range(4):
                        for ck in range(qt + 1):
                            k0, k1 = 512 * ck, min(512 * ck + 512, nk)
                            r = nmx[0] % 2
                            nmx[0] += 1
                            diag = k1 == nk
                            if stacked.get(hg) is None:
                                raise ValueError("not stacked")
                            k = p.mm(mbank[r][:, 0:k1 - k0], qp[i][0:96, j, q0:q0 + 128], kp[i][0:96, j, k0:k1], True,
                                     not diag, m_free[r], *stacked[hg], sig=not diag)
                            if diag:
                                k = p.mm(mbank[r][:, k1 - k0 - 128:k1 - k0], p.idb[:, :], p.mS[:, :], False, True, sig=True)
                            out, x = pm[g][:, 4 * qb + j, ck:ck + 1], mbank[r][:, 0:k1 - k0]
                            m_free[r] = dve.do(lambda e, out=out, x=x: e.reduce_max(out, x, AX.X), k, pm_free[g])
                            cnt += 1
                            if pend is not None and cnt == 3:
                                pend()
                                pend = None
                            yield (hg, qt)
                pend = combine(hg, qt, g, m_free)
        pend()
        yield (3, 3)

    def combine(hg, qt, g, m_free):
        out, x = nm[g][:, :, :].rearrange("p a b -> p (a b)"), pm[g][:, :, 0:qt + 1]
        k = dve.do(lambda e: e.reduce_max(out, x, AX.X, negate=True), dve.last(), nm_free[g])
        pm_free[g] = k
        k = p.cp(dve, mc[g][:, :, 0:4], nm[g][:, :, :], k, mc_free[g])
        kd = p.tt(dve, mc[g][:, :, 4:8], nm[g][:, :, :], mc[g][:, :, 0:4], ALU.subtract, k)
        nm_free[g] = kd

        def rows():
            r = nmx[0] % 2
            nmx[0] += 1
            for qb in range(4):
                k = p.mm(mbank[r][96:128, 128 * qb:128 * qb + 128], mc[g][:, qb, :], p.idh[:, :], True, True, kd,
                         m_free[r], sig=qb == 3)
            mc_free[g] = k
            q = slice(512 * qt, 512 * qt + 512)
            i = hg % 2
            k = p.af(qp[i][96:128, 0, q], mbank[r][96:128, :], ACT.Copy, k, last_use.get(hg - 2))
            m_free[r] = k
            k2 = p.cp(pool, qp[i][96:128, 1:4, q], qp[i][96:128, 0:1, q].broadcast_to([32, 3, 512]), k)
            biased[(hg, qt)] = (k, k2)
        return rows

    gen = max_units()
    state = {"done": (0, -1)}

    def advance(n):
        for _ in range(n):
            try:
                state["done"] = next(gen)
            except StopIteration:
                return

    def until(hg, qt):
        while (hg, qt) not in biased:
            next(gen)

    steps = [(hg, qt, kt) for hg in range(4) for qt in range(4) for kt in range(4 * qt + 4)]
    st_free = [None, None]
    e_free = [None, None]
    exp_ready = {}
    av_free = [None]

    def score(n, h):
        hg, qt, kt = steps[n]
        i = hg % 2
        off = max(0, kt - 4 * qt) * 128
        for jj in range(2):
            j = 2 * h + jj
            diag = kt >= 4 * qt
            k = p.mm(st[h][:, jj, off:512], kp[i][:, j, 128 * kt:128 * kt + 128],
                     qp[i][:, j, 512 * qt + off:512 * qt + 512], True, not diag, st_free[h], kc[i], *biased[(hg, qt)],
                     sig=jj == 1 and not diag)
            if diag:
                k = p.mm(st[h][:, jj, off:off + 128], p.idb[:, :], p.mT[:, :], False, True, sig=jj == 1)
        st_free[h] = p.af(E[n % 2][:, 2 * h:2 * h + 2, off:512], st[h][:, :, off:512], ACT.Exp, k, e_free[n % 2])
        exp_ready[(n, h)] = st_free[h]
        last_use[hg] = k

    def weigh(n):
        hg, qt, kt = steps[n]
        off = max(0, kt - 4 * qt) * 128
        first, last = kt == 0, kt == 4 * qt + 3
        for j in range(4):
            h = 4 * hg + j
            p.mm(AV[32 * j:32 * j + 32, off:512], p.v[:, kt, 32 * h:32 * h + 32], E[n % 2][:, j, off:512], first, last,
                 exp_ready[(n, j // 2)], av_free[0])
        for j in range(4):
            k = p.mm(RS[32 * j:32 * j + 32, off:512], p.ones[:, :], E[n % 2][:, j, off:512], first, last, sig=j == 3)
        e_free[n % 2] = k
        if last:
            k = dve.do(lambda e: e.reciprocal(rec[:, :], RS), k, av_free[0])
            av_free[0] = p.tt(dve, avn[:, hg, 512 * qt:512 * qt + 512], AV, rec[:, :], ALU.mult, k)

    restack(0)
    restack(1)
    p.pe.need(*kc)
    advance(24)
    nstack = 2
    for n, (hg, qt, kt) in enumerate(steps):
        if kt == 0:
            until(hg, qt)
        rate = 5 if n % 40 < 24 and hg == 0 else 4
        score(n, 0)
        if qt == 3 and kt == 15 and hg + 2 < 4:
            pass
        advance(rate // 2)
        score(n, 1)
        if n:
            weigh(n - 1)
        if kt == 15 and hg + 2 < 4:
            restack(hg + 2)
        advance(rate - rate // 2)
    weigh(len(steps) - 1)


def outproj(p, b):
    pe, dve, act, pool = p.pe, p.dve, p.act, p.pool
    o = 106496
    wh, wl = p.at([128, KC, D], F32R, o), p.at([128, KC, D], F32R, o + 8192)
    wraw = p.at([128, KC, D], F32, o + 16384)
    o += 24576
    ah = [p.at([128, KC, 512], F32R, o + 16384 * i) for i in range(2)]
    al = [p.at([128, KC, 512], F32R, o + 16384 * i + 8192) for i in range(2)]
    o += 32768
    xr = [p.at([128, 512], F32, o + 2048 * i) for i in range(4)]
    avn = p.qs[:, :, :, :].rearrange("p g a s -> p g (a s)").bitcast(F32)
    k = p.dma.go(wraw[:, :, :], p.a["L0_attn_Wo"].rearrange("(c p) n -> p c n", p=128))
    k = p.cp(dve, wh[:, :, :], wraw[:, :, :], k)
    kw = p.tt(dve, wl[:, :, :], wraw[:, :, :], wh[:, :, :], ALU.subtract, k)
    src = p.xa[S * b:S * (b + 1), :].rearrange("(n t p) d -> n t p d", t=4, p=128)
    dst = p.xc[S * b:S * (b + 1), :].rearrange("(n t p) d -> n t p d", t=4, p=128)
    a_free, ring_free, xr_free = [None] * 2, [None] * 8, [None] * 4
    n = 0
    for q in range(4):
        i = q % 2
        x = avn[:, :, 512 * q:512 * q + 512]
        k = p.cp(dve, ah[i][:, :, :], x, a_free[i])
        ka = p.tt(dve, al[i][:, :, :], x, ah[i][:, :, :], ALU.subtract, k)
        for tb in range(4):
            r, s = n % 8, n % 4
            n += 1
            c0 = slice(128 * tb, 128 * tb + 128)
            kx = p.dma.go(xr[s][:, :], src[q, tb], xr_free[s])
            kx = p.tt(pool, xr[s][:, :], xr[s][:, :], p.bob[:, :], ALU.add, kx)
            for c in range(KC):
                p.mm(p.b[r], ah[i][:, c, c0], wh[:, c, :], c == 0, False, ring_free[r], ka, kw)
                p.mm(p.b[r], ah[i][:, c, c0], wl[:, c, :], False, False)
                k = p.mm(p.b[r], al[i][:, c, c0], wh[:, c, :], False, c == KC - 1, sig=c == KC - 1)
            ring_free[r] = p.tt(dve, xr[s][:, :], p.b[r], xr[s][:, :], ALU.add, k, kx)
            xr_free[s] = p.dma.go(dst[q, tb], xr[s][:, :], ring_free[r])
        a_free[i] = k


def program(nc, a):
    p = Prog(nc, a)
    p.xa = nc.dram_tensor("xa", [T, D], F32).ap()
    p.xc = nc.dram_tensor("xc", [T, D], F32).ap()
    p.dga, p.dgb = (nc.dram_tensor(n, [128, 11264], F32).ap() for n in ("dga", "dgb"))
    p.dda, p.ddb = (nc.dram_tensor(n, [128, 5632], F32).ap() for n in ("dda", "ddb"))
    psum(p)
    constants(p)
    ffn_memory(p)
    dequant(p)
    p.barrier()
    ffn(p, a["L0_attn_X"].rearrange("b s d -> (b s) d"), p.xa, spill_views(p))
    p.barrier()
    p.qs = p.at([128, 4, 2, S], F16, 8192)
    p.ks = p.at([128, 4, 2, S], F16, 40960)
    p.v = p.at([128, 16, D], F32, 73728)
    for b in range(B):
        qkv(p, b)
        p.barrier()
        attention(p, b)
        p.barrier()
        outproj(p, b)
        p.barrier()
    for w in spill_views(p):
        for s, d in w:
            p.dma.go(s, d)
    p.barrier()
    ffn(p, p.xc, a["out"].rearrange("b s d -> (b s) d"), None)
    p.barrier()
    with nc.Block() as block:
        @block.sync
        def _(e):
            p.sp.run(e)

        @block.tensor
        def _(e):
            p.pe.run(e)

        @block.vector
        def _(e):
            p.dve.run(e)

        @block.scalar
        def _(e):
            p.act.run(e)

        @block.gpsimd
        def _(e):
            p.pool.run(e)


_INS = ["L0_attn_X", "L0_attn_ln_g", "L0_attn_ln_b", "L0_attn_Wq", "L0_attn_bq", "L0_attn_Wk", "L0_attn_bk",
        "L0_attn_Wv", "L0_attn_bv", "L0_attn_Wo", "L0_attn_bo", "L0_ffn_gate_up_packed", "L0_ffn_gate_up_scales",
        "L0_ffn_down_packed", "L0_ffn_down_scales"]


def kernel(**inputs):
    import numpy as np
    import concourse.bacc as bacc
    from concourse.bass_utils import run_bass_kernel_spmd

    nc = bacc.Bacc("TRN2", target_bir_lowering=False, num_devices=1)
    arrays, a = {}, {}
    for name in _INS:
        x = np.ascontiguousarray(inputs[name])
        arrays[name] = x
        a[name] = nc.dram_tensor(name, x.shape, mybir.dt.from_np(x.dtype), kind="ExternalInput").ap()
    a["out"] = nc.dram_tensor("out", (B, S, D), F32, kind="ExternalOutput").ap()
    program(nc, a)
    r = run_bass_kernel_spmd(nc, [arrays], core_ids=[0])
    return r.results[0]["out"]
```

```python
import concourse.bass as bass
import concourse.mybir as mybir

F32 = mybir.dt.float32
F32R = mybir.dt.float32r
F16 = mybir.dt.float16
BF16 = mybir.dt.bfloat16
I32 = mybir.dt.int32
U16 = mybir.dt.uint16
ALU = mybir.AluOpType
ACT = mybir.ActivationFunctionType
AX = mybir.AxisListType

B, S, D, H, DH = 2, 2048, 512, 16, 32
T = B * S
I = 1408
IC = I // 128
KC = D // 128
NT = T // 512
SC = float(1.0 / (32.0 ** 0.5))
NEG = -1.0e30
BASE = 16512
C0 = 7936
WD0 = C0 + 90112
X0 = WD0 + 45056
H0 = X0 + 32768
XB0 = H0 + 20480
XR0 = XB0 + 8192
QS0 = WD0
KP0 = C0 + 65536


class Lane:

    def __init__(self, nc, name):
        self.nc, self.name = nc, name
        self.items, self.seen = [], {}
        self.phase = 0
        self.fresh()

    def fresh(self):
        self.sem = self.nc.alloc_semaphore(f"{self.name}{self.phase}")
        self.key = f"{self.name}{self.phase}"
        self.phase += 1
        self.n = 0

    def need(self, *toks):
        for t in toks:
            if t is None:
                continue
            key, sem, value = t
            if self.seen.get(key, 0) >= value:
                continue
            self.seen[key] = value
            self.items.append(lambda e, sem=sem, value=value: e.wait_ge(sem, value))

    def do(self, fn, *toks, sig=True):
        self.need(*toks)
        if not sig:
            self.items.append(fn)
            return None
        self.n += 1
        sem = self.sem
        self.items.append(lambda e: fn(e).then_inc(sem, 1))
        return (self.key, sem, self.n)

    def last(self):
        return (self.key, self.sem, self.n) if self.n else None

    def run(self, e):
        for f in self.items:
            f(e)


class Dma:

    N = 32

    def __init__(self, nc, sp):
        self.sp = sp
        self.sems = [nc.alloc_semaphore(f"dma{i}") for i in range(self.N)]
        self.count = [0] * self.N
        self.i = 0

    def go(self, dst, src, *toks):
        k = self.i % self.N
        self.i += 1
        sem = self.sems[k]
        if self.count[k]:
            self.sp.need((f"dma{k}", sem, self.count[k]))
        self.count[k] += 16
        self.sp.need(*toks)
        self.sp.items.append(lambda e: e.dma_start(dst, src).then_inc(sem, 16))
        return (f"dma{k}", sem, self.count[k])

    def all(self):
        return [(f"dma{k}", self.sems[k], c) for k, c in enumerate(self.count) if c]


class Prog:
    def __init__(self, nc, a):
        self.nc, self.a = nc, a
        self.pe, self.dve, self.act = Lane(nc, "pe"), Lane(nc, "dve"), Lane(nc, "act")
        self.pool, self.sp = Lane(nc, "pool"), Lane(nc, "sp")
        self.lanes = [self.pe, self.dve, self.act, self.pool, self.sp]
        self.dma = Dma(nc, self.sp)
        self.nuid = 0

    def at(self, shape, dt, off):
        self.nuid += 1
        return self.nc.alloc_sbuf_tensor_at(f"sb{self.nuid}", list(shape), dt, offset=BASE + off)

    def barrier(self):
        toks = [ln.last() for ln in self.lanes] + self.dma.all()
        for ln in self.lanes:
            ln.need(*toks)
        for ln in self.lanes:
            ln.fresh()

    def mm(self, out, l, r, st, sp, *toks, sig=False):
        return self.pe.do(lambda e: e.matmul(out, l, r, start=st, stop=sp), *toks, sig=sig)

    def tr(self, out, x, ident, *toks, sig=False):
        return self.pe.do(lambda e: e.transpose(out, x, ident), *toks, sig=sig)

    def af(self, out, x, func, *toks, **kw):
        return self.act.do(lambda e: e.activation(out, x, func, **kw), *toks)

    def tt(self, ln, out, x, y, op, *toks):
        return ln.do(lambda e: e.tensor_tensor(out, x, y, op), *toks)

    def ts(self, ln, out, x, s1, s2, op0, op1, *toks):
        if op1 is None:
            return ln.do(lambda e: e.tensor_scalar(out, x, s1, None, op0), *toks)
        return ln.do(lambda e: e.tensor_scalar(out, x, s1, s2, op0, op1), *toks)

    def stt(self, out, x, s, y, op0, op1, *toks):
        return self.dve.do(lambda e: e.scalar_tensor_tensor(out, x, s, y, op0, op1), *toks)

    def cp(self, ln, out, x, *toks):
        return ln.do(lambda e: e.tensor_copy(out, x), *toks)

    def rsqrt(self, out, x, scale, eps, mult, w, *toks):
        v, g, t = w[:, 0, :], w[:, 1, :], w[:, 2, :]
        d = self.dve
        k = self.ts(d, v, x, scale / mult ** 2, eps / mult ** 2, ALU.mult, ALU.add, *toks)
        k = self.ts(d, t.bitcast(I32), v.bitcast(I32), 1, None, ALU.logical_shift_right, None, k)
        k = self.ts(d, g.bitcast(I32), t.bitcast(I32), -1.0, float(0x5F3759DF), ALU.mult, ALU.add, k)
        for n in range(3):
            k = self.tt(d, t, g, g, ALU.mult, k)
            k = self.stt(t, t, -0.5, v, ALU.mult, ALU.mult, k)
            k = self.stt(out if n == 2 else g, t, 1.5, g, ALU.add, ALU.mult, k)
        return k


def constants(p):
    o = 0

    def take(shape, dt, size):
        nonlocal o
        t = p.at(shape, dt, o)
        o += (size + 31) // 32 * 32
        return t

    p.idf = take([128, 128], F32, 512)
    p.idh = take([128, 128], F16, 256)
    p.idb = take([128, 128], BF16, 256)
    p.mS = take([128, 128], BF16, 256)
    p.mT = take([128, 128], BF16, 256)
    p.ones = take([128, 32], F32, 128)
    p.st = take([128, 4, 6], F32, 96)
    p.mv = take([128, 4, 2], F32, 32)
    p.rs = take([128, 4], F32, 32)
    p.w4 = take([128, 3, 4], F32, 48)
    p.ss = take([128, 4], F32, 32)
    p.r4 = take([128, 4], F32, 32)
    p.w5 = take([128, 3, 4], F32, 48)
    p.st2 = take([128, 4, 6], F32, 96)
    p.mv2 = take([128, 4, 2], F32, 32)
    p.rs2 = take([128, 4], F32, 32)
    p.bias = take([128, 4, 4], F32, 64)
    p.bvb = take([128, 512], F32, 2048)
    p.bob = take([128, 512], F32, 2048)
    p.sg = take([128, 22, 4], F32, 352)
    p.sd = take([128, 4, 11], F32, 176)
    p.junk = take([128, 512], BF16, 1024)
    assert o <= C0
    a, pool = p.a, p.pool
    k0 = pool.do(lambda e: e.memset(p.idf[:, :], 0.0))
    k1 = pool.do(lambda e: e.memset(p.mS[:, :], 0.0))
    k2 = pool.do(lambda e: e.memset(p.mT[:, :], 0.0))
    pool.do(lambda e: e.memset(p.ones[:, :], 1.0))
    p.kid = pool.do(lambda e: e.affine_select(out=p.idf[:, :], in_=p.idf[:, :], compare_op=ALU.not_equal, fill=1.0,
                                              base=0, pattern=[[-1, 128]], channel_multiplier=1), k0)
    pool.do(lambda e: e.affine_select(out=p.mS[:, :], in_=p.mS[:, :], compare_op=ALU.is_ge, fill=NEG,
                                      base=0, pattern=[[-1, 128]], channel_multiplier=1), k1)
    pool.do(lambda e: e.affine_select(out=p.mT[:, :], in_=p.mT[:, :], compare_op=ALU.is_ge, fill=NEG,
                                      base=0, pattern=[[1, 128]], channel_multiplier=-1), k2)
    p.cp(pool, p.idh[:, :], p.idf[:, :], p.kid)
    p.cp(pool, p.idb[:, :], p.idf[:, :], p.kid)


def attention_vectors(p):
    a = p.a
    rows = p.at([16, 128], F32, XR0)
    ks = [p.dma.go(rows[4 * n:4 * n + 4, :], a[f"L0_attn_{name}"].rearrange("(c p) -> c p", p=128))
          for n, name in enumerate(("ln_g", "ln_b", "bq", "bk"))]
    k = p.tr(p.b[7][:, 0:16], rows[:, :], p.idf[0:16, 0:16], *ks, sig=True)
    k = p.cp(p.dve, p.bias[:, :, :].rearrange("p a b -> p (a b)"), p.b[7][:, 0:16], k)
    p.ts(p.dve, p.bias[:, 2, :], p.bias[:, 2, :], SC, None, ALU.mult, None, k)
    p.dma.go(p.bvb[:, :], a["L0_attn_bv"].partition_broadcast(128))
    p.dma.go(p.bob[:, :], a["L0_attn_bo"].partition_broadcast(128))


def psum(p):
    p.bank = [p.nc.alloc_psum_tensor(f"ps{i}", [128, 512], F32) for i in range(2)]
    p.pair = [p.nc.alloc_psum_tensor(f"pp{i}", [128, 2, 512], F32) for i in range(3)]
    p.b = [p.bank[0][:, :], p.bank[1][:, :]] + [p.pair[i][:, n, :] for i in range(3) for n in range(2)]


def ffn_memory(p):
    p.wga, p.wgb = (p.at([128, IC, KC, 2, 128], F32R, C0 + 45056 * i) for i in range(2))
    p.wda, p.wdb = (p.at([128, IC, D], F32R, WD0 + 22528 * i) for i in range(2))
    p.x1 = [p.at([128, KC, 512], F32R, X0 + 16384 * i) for i in range(2)]
    p.x2 = [p.at([128, KC, 512], F32R, X0 + 16384 * i + 8192) for i in range(2)]
    p.h1 = [p.at([128, 512], F32R, H0 + 2048 * i) for i in range(3)]
    p.h2 = [p.at([128, 512], F32R, H0 + 6144 + 2048 * i) for i in range(3)]
    p.sil = [p.at([128, 512], F32, H0 + 12288 + 2048 * i) for i in range(2)]
    p.h = [p.at([128, 512], F32, H0 + 16384 + 2048 * i) for i in range(2)]
    p.xb = [p.at([128, 512], F32, XB0 + 2048 * i) for i in range(4)]
    p.xr = [p.at([128, 512], F32, XR0 + 2048 * i) for i in range(4)]


class Dequant:

    def __init__(self, p):
        self.p = p
        a, dve = p.a, p.dve
        o = X0 + 16384
        self.pk = p.at([128, IC, 192], I32, o)
        self.v = p.at([128, 4, 768], U16, o + 8448)
        self.w32 = [p.at([128, 4, 128], F32, XR0 + 2048 * i) for i in range(2)]
        self.t1 = [p.at([128, 768], U16, XR0 + 4096 + 1536 * i) for i in range(2)]
        sc16 = p.at([11, 2816 + 512], F16, WD0 + 13312)
        sc32 = p.at([11, 2816 + 512], F32, WD0)
        gu = a["L0_ffn_gate_up_packed"].rearrange("(u i p) w -> u p i w", u=2, p=128)
        ks1 = p.dma.go(sc16[0:4, 0:2816], a["L0_ffn_gate_up_scales"])
        ks2 = p.dma.go(sc16[0:11, 2816:3328], a["L0_ffn_down_scales"])
        self.kpk = [p.dma.go(self.pk[:, :, 64 * u:64 * u + 64], gu[u]) for u in range(2)]
        dn = a["L0_ffn_down_packed"].rearrange("(h p) (i w) -> h p i w", p=128, w=16)
        self.kpk += [p.dma.go(self.pk[:, :, 128 + 16 * h:144 + 16 * h], dn[h]) for h in range(4)]
        c1 = p.af(sc32[0:4, 0:2816], sc16[0:4, 0:2816], ACT.Copy, ks1, scale=16384.0)
        c2 = p.af(sc32[0:11, 2816:3328], sc16[0:11, 2816:3328], ACT.Copy, ks2, scale=16384.0)
        for t in range(22):
            k1 = p.tr(p.b[4][:, 4 * t:4 * t + 4], sc32[0:4, 128 * t:128 * t + 128], p.idf[0:4, 0:4], p.kid, c1,
                      sig=t == 21)
        for t in range(4):
            k2 = p.tr(p.b[5][:, 11 * t:11 * t + 11], sc32[0:11, 2816 + 128 * t:2944 + 128 * t], p.idf[0:11, 0:11], c2,
                      sig=t == 3)
        self.e1 = p.af(p.sg[:, :, :].rearrange("p a b -> p (a b)"), p.b[4][:, 0:88], ACT.Copy, k1)
        self.e2 = p.af(p.sd[:, :, :].rearrange("p a b -> p (a b)"), p.b[5][:, 0:44], ACT.Copy, k2)
        self.t_free = [None, None]
        self.v_free = None
        self.w_free = [None, None]
        self.n = 0
        self.kd = {}

    def decode(self, i0, i1):
        p, dve = self.p, self.p.dve
        n = 384 * (i1 - i0)
        u = self.pk[:, :, :].rearrange("p a b -> p (a b)").bitcast(U16)[:, 384 * i0:384 * i1]
        pend, done = [], None
        for m in range(5):
            if m < 4:
                t, v = self.t1[m % 2][:, 0:n], self.v[:, m, 0:n]
                p.ts(dve, t, u, 12 - 4 * m, 0x8000, ALU.logical_shift_left, ALU.bitwise_and, self.t_free[m % 2],
                     *self.kpk)
                sh = 9 - 4 * m
                op = ALU.logical_shift_left if sh >= 0 else ALU.logical_shift_right
                k = p.ts(dve, v, u, abs(sh), 0x0E00, op, ALU.bitwise_and, self.v_free)
                pend.append((m, t, v, k))
            if m >= 1:
                j, t, v, k = pend.pop(0)
                done = self.t_free[j % 2] = p.tt(dve, v, v, t, ALU.bitwise_or, k)
        for i in range(i0, i1):
            self.kd[i] = (384 * (i - i0), done)

    def scaled(self, i, part):
        p = self.p
        at, k = self.kd[i]
        v = self.v[:, :, at + 128 * part:at + 128 * part + 128].bitcast(F16).rearrange("p b (g q) -> p g q b", g=4)
        s = p.sg[:, IC * part + i, :] if part < 2 else p.sd[:, :, i]
        s = s.unsqueeze(2).unsqueeze(3).broadcast_to([128, 4, 32, 4])
        r = self.n % 2
        self.n += 1
        w = self.w32[r]
        k = p.tt(p.pool, w[:, :, :].rearrange("p g (q b) -> p g q b", b=4), v, s, ALU.mult, k, self.e1, self.e2,
                 self.w_free[r])
        self.v_free = k
        return r, k

    def turned(self, i, part, r, kw, free):
        p = self.p
        bk = p.b[0]
        for g in range(4):
            k = p.tr(bk[:, 128 * g:128 * g + 128], self.w32[r][:, g, :], p.idf[:, :], kw, free, sig=g == 3)
        self.w_free[r] = k
        if part < 2:
            oa, ob = p.wga[:, i, :, part, :], p.wgb[:, i, :, part, :]
            bk = bk.rearrange("p (g o) -> p g o", g=4)
        else:
            oa, ob = p.wda[:, i, :], p.wdb[:, i, :]
        k = p.af(oa, bk, ACT.Copy, k)
        return p.tt(p.dve, ob, bk, oa, ALU.subtract, k)


def weight_pieces(p):
    out = []
    for i in range(IC):
        row = [(w[:, i, :, :, :].rearrange("p a b c -> p (a b c)").bitcast(F32), d[i]) for w, d in
               ((p.wga, p.dga), (p.wgb, p.dgb))]
        row += [(w[:, i, :].bitcast(F32), d[i]) for w, d in ((p.wda, p.dda), (p.wdb, p.ddb))]
        out.append(row)
    return out


def ffn(p, src, dst, deq=None, loaded=None):
    pe, dve, act, pool = p.pe, p.dve, p.act, p.pool
    TB = p.b[0]
    ring = [p.b[1], p.b[2], p.b[3]]
    Y = p.b[4:8]
    srcv = src.rearrange("(n t p) d -> n t p d", t=4, p=128)
    dstv = dst.rearrange("(n t p) d -> n t p d", t=4, p=128)
    pieces = weight_pieces(p)
    st = {"tb": None, "mv": None, "r4": None}
    xb_free, x_free, x_ready, kx = [None] * 4, [None, None], {}, {}
    ring_free, nring = [None] * 3, [0]
    sil_free, h_free, hh_free, h_ready = [None] * 2, [None] * 2, [None] * 3, {}
    y_free, ky, xr_free, kr = [None] * 4, [None] * 4, [None] * 4, {}
    if deq is not None:
        kg, kdn = {}, {}
        x_free[1] = None
    else:
        kg, kdn = loaded

    def load(tt):
        kx[tt] = [p.dma.go(p.xb[tb][:, :], srcv[tt, tb], xb_free[tb]) for tb in range(4)]

    def stats(tt):
        ks = []
        for tb in range(4):
            o, x, m = p.st[:, tb, :], p.xb[tb][:, :], p.mv[:, tb, :]
            k = dve.do(lambda e, o=o, x=x: e.bn_stats(o, x), kx[tt][tb])
            ks.append(dve.do(lambda e, o=o, m=m: e.bn_aggr(m, o), k, st["mv"]))
        k = p.rsqrt(p.rs[:, :], p.mv[:, :, 1], 1.0, 1e-5, 1.0, p.w4, *ks)
        out = [p.ts(dve, p.xb[tb][:, :], p.xb[tb][:, :], p.mv[:, tb, 0:1], p.rs[:, tb:tb + 1],
                    ALU.subtract, ALU.mult, k) for tb in range(4)]
        st["mv"] = out[3]
        return out

    def chunk(tt, c, kn):
        for tb in range(4):
            k = p.tr(TB[:, 128 * tb:128 * tb + 128], p.xb[tb][:, 128 * c:128 * c + 128], p.idf[:, :], kn[tb],
                     st["tb"], sig=tb == 3)
        if c == 3:
            xb_free[:] = [k] * 4
        i = tt % 2
        ka = p.af(p.x1[i][:, c, :], TB, ACT.Copy, k, x_free[i])
        st["tb"] = x_ready[tt] = p.tt(dve, p.x2[i][:, c, :], TB, p.x1[i][:, c, :], ALU.subtract, ka)

    def proj(tt, i, u):
        r = nring[0] % 3
        nring[0] += 1
        x1, x2 = p.x1[tt % 2], p.x2[tt % 2]
        for c in range(KC):
            p.mm(ring[r], p.wga[:, i, c, u, :], x1[:, c, :], c == 0, False, ring_free[r], x_ready[tt], *kg[i])
            p.mm(ring[r], p.wga[:, i, c, u, :], x2[:, c, :], False, False)
            k = p.mm(ring[r], p.wgb[:, i, c, u, :], x1[:, c, :], False, c == KC - 1, sig=c == KC - 1)
        return r, k

    def up(tt, i):
        u = tt * IC + i
        s, h, h1, h2 = p.sil[u % 2], p.h[u % 2], p.h1[u % 3], p.h2[u % 3]
        turn = deq is not None and tt == 0 and i + 1 < IC

        def weights(part):
            if turn:
                r, k = todo[(i + 1, part)]
                k = deq.turned(i + 1, part, r, k, st["tb"])
                st["tb"] = k
                (kg if part < 2 else kdn).setdefault(i + 1, []).append(k)

        if turn:
            if i % 2 == 0:
                deq.decode(i + 1, min(i + 3, IC))
            for part in range(2):
                todo[(i + 1, part)] = deq.scaled(i + 1, part)
        rg, k = proj(tt, i, 0)
        weights(0)
        ks = p.af(s[:, :], ring[rg], ACT.Silu, k, sil_free[u % 2])
        ring_free[rg] = ks
        ru, k = proj(tt, i, 1)
        if i == IC - 1:
            x_free[tt % 2] = k
        weights(1)
        if turn:
            todo[(i + 1, 2)] = deq.scaled(i + 1, 2)
        kh = p.tt(dve, h[:, :], s[:, :], ring[ru], ALU.mult, ks, k, h_free[u % 2])
        ring_free[ru] = sil_free[u % 2] = kh
        k1 = p.af(h1[:, :], h[:, :], ACT.Copy, kh, hh_free[u % 3])
        h_free[u % 2] = h_ready[u] = p.tt(dve, h2[:, :], h[:, :], h1[:, :], ALU.subtract, k1)
        return weights

    def down(tt, i):
        u = tt * IC + i
        h1, h2 = p.h1[u % 3], p.h2[u % 3]
        for tb in range(4):
            c = slice(128 * tb, 128 * tb + 128)
            last = i == IC - 1
            p.mm(Y[tb], h1[:, c], p.wda[:, i, :], i == 0, False, h_ready[u], y_free[tb], *kdn[i])
            p.mm(Y[tb], h1[:, c], p.wdb[:, i, :], False, False)
            k = p.mm(Y[tb], h2[:, c], p.wda[:, i, :], False, last, sig=last or tb == 3)
            if last:
                ky[tb] = k
        hh_free[u % 3] = k

    def residual(tt):
        kr[tt] = [p.dma.go(p.xr[tb][:, :], srcv[tt, tb], xr_free[tb]) for tb in range(4)]

    def finish(tt):
        ks = []
        for tb in range(4):
            o = p.ss[:, tb:tb + 1]
            ks.append(p.af(p.junk[:, :], Y[tb], ACT.Square, ky[tb], st["r4"], act.last(), accum_out=o))
        k = p.rsqrt(p.r4[:, :], p.ss[:, :], 1.0 / D, 1e-6, 0.5, p.w5, *ks)
        for tb in range(4):
            x = p.xr[tb][:, :]
            ko = p.stt(x, Y[tb], p.r4[:, tb:tb + 1], x, ALU.mult, ALU.add, kr[tt][tb], k)
            y_free[tb] = st["r4"] = ko
            xr_free[tb] = p.dma.go(dstv[tt, tb], x, ko)

    todo = {}
    load(0)
    if deq is not None:
        deq.decode(0, 1)
        for part in range(3):
            todo[(0, part)] = deq.scaled(0, part) if part < 2 else None
    kn = stats(0)
    for c in range(KC):
        chunk(0, c, kn)
    load(1)
    if deq is not None:
        for part in range(3):
            r, k = todo[(0, part)] or deq.scaled(0, part)
            k = deq.turned(0, part, r, k, st["tb"])
            st["tb"] = k
            (kg if part < 2 else kdn).setdefault(0, []).append(k)
    for tt in range(NT):
        late = 2 if deq is not None and tt == 0 else 0
        for i in range(IC):
            weights = up(tt, i)
            if i == 0 and tt:
                down(tt - 1, IC - 1)
                finish(tt - 1)
            elif i == 2:
                down(tt, 0)
                down(tt, 1)
            elif i > 2:
                down(tt, i - 1)
            weights(2)
            if tt + 1 < NT:
                if i == 3 + late:
                    kn = stats(tt + 1)
                if i in (4, 5, 6, 7) and not late:
                    chunk(tt + 1, i - 4, kn)
                if i == 10 and late:
                    x_free[1] = deq.v_free
                    for c in range(KC):
                        chunk(tt + 1, c, kn)
            if i == 8 and not late or i == 10 and late:
                if late:
                    xr_free[:] = [st["tb"]] * 4
                residual(tt)
                if tt + 2 < NT:
                    load(tt + 2)
            if deq is not None and tt in (2, 3, 4, 5) and i >= 3:
                for s, d in pieces[i - 3 + 8 * (tt - 2)] if i - 3 + 8 * (tt - 2) < IC else ():
                    p.dma.go(d, s)
    down(NT - 1, IC - 1)
    finish(NT - 1)


def qkv(p, b):
    pe, dve, act, pool = p.pe, p.dve, p.act, p.pool
    a = p.a
    o = QS0 + 32768
    wh = [p.at([128, KC, D], F32R, o + 16384 * i) for i in range(3)]
    wl = [p.at([128, KC, D], F32R, o + 16384 * i + 8192) for i in range(3)]
    o += 49152
    xb = [p.at([128, 512], F32, o + 2048 * i) for i in range(4)]
    xnt = [p.at([128, 512], F32, o + 8192 + 2048 * i) for i in range(2)]
    q32 = [p.at([128, 512], F32, o + 12288 + 2048 * i) for i in range(2)]
    o += 16384
    xo = [KP0, o]
    xh = [p.at([128, KC, 512], F32R, xo[i]) for i in range(2)]
    xl = [p.at([128, KC, 512], F32R, xo[i] + 8192) for i in range(2)]
    wraw = [p.at([128, KC, D], F32, xo[1] + 8192 * i) for i in range(2)]
    srcv = p.xa[S * b:S * (b + 1), :].rearrange("(n t p) d -> n t p d", t=4, p=128)
    tbank = [p.b[0], p.b[1]]
    t_free = [None, None]
    ring = p.b[2:8]
    ring_free, nr = [None] * 6, [0]
    xb_free = [None] * 4
    xnt_free, q32_free, x_free = [None] * 2, [None] * 2, [None] * 2
    s_free = [None, None]
    x_ready, kx, kn = {}, {}, {}
    nx, nq = [0], [0]
    kw = []

    def load(tt):
        kx[tt] = [p.dma.go(xb[tb][:, :], srcv[tt, tb], xb_free[tb]) for tb in range(4)]

    def norm(tt, rnd):
        st, mv, rs, w = (p.st, p.mv, p.rs, p.w4) if rnd == 0 else (p.st2, p.mv2, p.rs2, p.w5)
        ks = []
        for tb in range(4):
            o_, x_, m_ = st[:, tb, :], xb[tb][:, :], mv[:, tb, :]
            k = dve.do(lambda e, o=o_, x=x_: e.bn_stats(o, x), kx[tt][tb])
            ks.append(dve.do(lambda e, o=o_, m=m_: e.bn_aggr(m, o), k, s_free[rnd]))
        k = p.rsqrt(rs[:, :], mv[:, :, 1], 1.0, 1e-5, 1.0, w, *ks)
        kx[tt] = [p.ts(dve, xb[tb][:, :], xb[tb][:, :], mv[:, tb, 0:1], rs[:, tb:tb + 1],
                       ALU.subtract, ALU.mult, k) for tb in range(4)]
        s_free[rnd] = kx[tt][3]

    def turn(tt, c):
        i, f, s = tt % 2, c % 2, c % 2
        for tb in range(4):
            k = p.tr(tbank[f][:, 128 * tb:128 * tb + 128], xb[tb][:, 128 * c:128 * c + 128], p.idf[:, :], kx[tt][tb],
                     t_free[f], sig=tb == 3)
        ka = t_free[f] = p.af(xnt[s][:, :], tbank[f], ACT.Identity, k, xnt_free[s], scale=p.bias[:, 0, c:c + 1],
                              bias=p.bias[:, 1, c:c + 1])
        kh = p.cp(dve, xh[i][:, c, :], xnt[s][:, :], ka, x_free[i])
        xnt_free[s] = x_ready[tt] = p.tt(dve, xl[i][:, c, :], xnt[s][:, :], xh[i][:, c, :], ALU.subtract, kh)
        if c == 3:
            xb_free[:] = [k] * 4

    def group(tt, lh, ll, rh, rl, k):
        r = nr[0] % 6
        nr[0] += 1
        for c in range(KC):
            p.mm(ring[r], lh(c), rh(c), c == 0, False, ring_free[r], x_ready[tt], k)
            p.mm(ring[r], lh(c), rl(c), False, False)
            k = p.mm(ring[r], ll(c), rh(c), False, c == KC - 1, sig=c == KC - 1)
        return r, k

    def features(tt, f, n):
        i = tt % 2
        ts_, fs = slice(512 * tt, 512 * tt + 512), slice(128 * f, 128 * f + 128)
        dst = (p.qs, p.ks)[n]
        r, k = group(tt, lambda c: wh[n][:, c, fs], lambda c: wl[n][:, c, fs], lambda c: xh[i][:, c, :],
                     lambda c: xl[i][:, c, :], kw[n])
        s = nq[0] % 2
        nq[0] += 1
        ka = ring_free[r] = p.af(q32[s][:, :], ring[r], ACT.Identity, k, q32_free[s], scale=SC if n == 0 else 1.0,
                                 bias=p.bias[:, 2 + n, f:f + 1])
        kh = p.cp(dve, dst[:, f, 0, ts_], q32[s][:, :], ka)
        q32_free[s] = p.tt(pool, dst[:, f, 1, ts_], q32[s][:, :], dst[:, f, 0, ts_], ALU.subtract, kh)

    def values(tt, tb):
        i = tt % 2
        c0 = slice(128 * tb, 128 * tb + 128)
        r, k = group(tt, lambda c: xh[i][:, c, c0], lambda c: xl[i][:, c, c0], lambda c: wh[2][:, c, :],
                     lambda c: wl[2][:, c, :], kw[2])
        ring_free[r] = p.tt(dve, p.v[:, 4 * tt + tb, :], ring[r], p.bvb[:, :], ALU.add, k)
        if tb == 3:
            x_free[i] = k

    load(0)
    wfree = [None, None]
    kraw = []
    for n, name in enumerate(("Wq", "Wk")):
        kraw.append(p.dma.go(wraw[n][:, :, :], a[f"L0_attn_{name}"].rearrange("(c p) n -> p c n", p=128)))
    norm(0, 0)
    norm(0, 1)
    for c in range(KC):
        turn(0, c)
    for n in range(3):
        w = wraw[n % 2]
        if n == 2:
            kraw.append(p.dma.go(w[:, :, :], a["L0_attn_Wv"].rearrange("(c p) n -> p c n", p=128), kw[0]))
        ka = p.af(wh[n][:, :, :], w[:, :, :], ACT.Copy, kraw[n])
        kw.append(p.tt(dve, wl[n][:, :, :], w[:, :, :], wh[n][:, :, :], ALU.subtract, ka))
    x_free[1] = kw[2]
    load(1)
    for tt in range(4):
        for g in range(8):
            features(tt, g // 2, g % 2)
            if tt < 3 and g in (1, 4):
                norm(tt + 1, g // 3)
        for tb in range(4):
            values(tt, tb)
            if tt < 3:
                turn(tt + 1, tb)
        if tt < 2:
            load(tt + 2)


def attention(p, b):
    pe, dve, act, pool = p.pe, p.dve, p.act, p.pool
    o = QS0 + 32768
    kp = [p.at([128, 4, S], F16, KP0), p.at([128, 4, S], F16, o)]
    qp = [p.at([128, 4, S], F16, o + 16384 + 16384 * i) for i in range(2)]
    o += 49152
    NE = 4
    E = [p.at([128, 4, 512], F32, o + 8192 * i) for i in range(NE)]
    o = KP0 + 16384
    rec = p.at([128, 512], F32, o)
    pm = [p.at([128, 16, 4], F32, o + 2048 + 256 * i) for i in range(2)]
    nm = [p.at([128, 4, 4], F32, o + 2560 + 64 * i) for i in range(2)]
    mc = [p.at([128, 4, 32], F16, o + 2688 + 256 * i) for i in range(2)]
    mbank = [p.b[0], p.b[1]]
    st = [p.pair[0], p.pair[1]]
    AV, RS = p.b[6], p.b[7]
    avn = p.qs[:, :, :, :].rearrange("p g a s -> p g (a s)").bitcast(F32)

    stacked, last_use = {}, {}

    def restack(hg):
        i = hg % 2
        ks = []
        for j in range(4):
            rows = slice(32 * j, 32 * j + 32)
            for r, (wk, wq) in enumerate(((0, 0), (1, 0), (0, 1))):
                at = slice(32 * r, 32 * r + 32)
                ks.append(p.dma.go(kp[i][at, j, :], p.ks[rows, hg, wk, :], last_use.get(hg - 2)))
                ks.append(p.dma.go(qp[i][at, j, :], p.qs[rows, hg, wq, :], last_use.get(hg - 2)))
        stacked[hg] = ks

    restack(0)
    kc = []
    k = None
    for i in range(2):
        k = pool.do(lambda e, x=kp[i]: e.memset(x[96:128, :, :], 0.0), k)
        for s in range(2):
            k = pool.do(lambda e, x=kp[i], s=s: e.affine_select(
                out=x[96:128, :, :], in_=x[96:128, :, :], compare_op=ALU.not_equal, fill=1.0, base=-4 * s,
                pattern=[[-1, 4], [0, S]], channel_multiplier=1), k)
        kc.append(k)
    mc_free = [act.do(lambda e, x=mc[i]: e.activation(x[:, :, :], p.mS[:, :].rearrange("p (a b) -> p a b", a=4),
                                                      ACT.Copy, scale=0.0)) for i in range(2)]
    pool.need(k)

    m_free, nmx = [None, None], [0]
    pm_free, nm_free, ngrp = [None, None], [None, None], [0]
    biased = {}

    def max_units():
        pend = None
        for hg in range(4):
            i = hg % 2
            for qt in range(4):
                g = ngrp[0] % 2
                ngrp[0] += 1
                cnt = 0
                for qb in range(4):
                    q0 = 512 * qt + 128 * qb
                    nk = q0 + 128
                    for j in range(4):
                        for ck in range(qt + 1):
                            k0, k1 = 512 * ck, min(512 * ck + 512, nk)
                            r = nmx[0] % 2
                            nmx[0] += 1
                            diag = k1 == nk
                            k = p.mm(mbank[r][:, 0:k1 - k0], qp[i][0:96, j, q0:q0 + 128], kp[i][0:96, j, k0:k1], True,
                                     not diag, m_free[r], *stacked[hg], sig=not diag)
                            if diag:
                                k = p.mm(mbank[r][:, k1 - k0 - 128:k1 - k0], p.idb[:, :], p.mS[:, :], False, True,
                                         sig=True)
                            out, x = pm[g][:, 4 * qb + j, ck:ck + 1], mbank[r][:, 0:k1 - k0]
                            m_free[r] = dve.do(lambda e, out=out, x=x: e.reduce_max(out, x, AX.X), k, pm_free[g])
                            cnt += 1
                            if pend is not None and cnt == 4:
                                pend()
                                pend = None
                            yield
                pend = combine(hg, qt, g)
        pend()
        yield

    def combine(hg, qt, g):
        out, x = nm[g][:, :, :].rearrange("p a b -> p (a b)"), pm[g][:, :, 0:qt + 1]
        k = dve.do(lambda e: e.reduce_max(out, x, AX.X, negate=True), dve.last(), nm_free[g])
        pm_free[g] = k
        k = p.cp(dve, mc[g][:, :, 0:4], nm[g][:, :, :], k, mc_free[g])
        kd = nm_free[g] = p.tt(dve, mc[g][:, :, 4:8], nm[g][:, :, :], mc[g][:, :, 0:4], ALU.subtract, k)

        def rows():
            r = nmx[0] % 2
            nmx[0] += 1
            for qb in range(4):
                k = p.mm(mbank[r][96:128, 128 * qb:128 * qb + 128], mc[g][:, qb, :], p.idh[:, :], True, True, kd,
                         m_free[r], sig=qb == 3)
            mc_free[g] = k
            q = slice(512 * qt, 512 * qt + 512)
            i = hg % 2
            k = m_free[r] = p.af(qp[i][96:128, 0, q], mbank[r][96:128, :], ACT.Copy, k, last_use.get(hg - 2))
            biased[(hg, qt)] = [k] + [p.dma.go(qp[i][96:128, j, q], qp[i][96:128, 0, q], k) for j in range(1, 4)]
        return rows

    gen = max_units()

    def advance(n):
        for _ in range(n):
            next(gen, None)

    steps = [(hg, qt, kt) for hg in range(4) for qt in range(4) for kt in range(4 * qt + 4)]
    st_free = [None, None]
    e_free, exp_ready, av_done, summed = [None] * NE, {}, {}, {}
    av_free, rs_free, rec_free = [None], [None], [None]
    copied = {}

    def offset(n):
        hg, qt, kt = steps[n]
        return max(0, kt - 4 * qt) * 128

    def score(n, h):
        hg, qt, kt = steps[n]
        i, off = hg % 2, offset(n)
        diag = kt >= 4 * qt
        for jj in range(2):
            j = 2 * h + jj
            k = p.mm(st[h][:, jj, off:512], kp[i][:, j, 128 * kt:128 * kt + 128],
                     qp[i][:, j, 512 * qt + off:512 * qt + 512], True, not diag, st_free[h], kc[i], *biased[(hg, qt)],
                     sig=jj == 1 and not diag)
            if diag:
                k = p.mm(st[h][:, jj, off:off + 128], p.idb[:, :], p.mT[:, :], False, True, sig=jj == 1)
        st_free[h] = exp_ready[(n, h)] = p.af(E[n % NE][:, 2 * h:2 * h + 2, off:512], st[h][:, :, off:512], ACT.Exp, k,
                                              e_free[n % NE])
        last_use[hg] = k

    def weigh(n):
        hg, qt, kt = steps[n]
        off = offset(n)
        for j in range(4):
            h = 4 * hg + j
            k = p.mm(AV[32 * j:32 * j + 32, off:512], p.v[:, kt, 32 * h:32 * h + 32], E[n % NE][:, j, off:512], kt == 0,
                     kt == 4 * qt + 3, exp_ready[(n, j // 2)], av_free[0], sig=j == 3)
        av_done[n] = k
        if kt == 4 * qt + 3:
            q = slice(512 * qt, 512 * qt + 512)
            av_free[0] = copied[(hg, qt)] = p.af(avn[:, hg, q], AV, ACT.Copy, k)
        if n % 2:
            for h in range(2):
                c = slice(2 * h, 2 * h + 2)
                summed[n] = p.tt(pool, E[(n - 1) % NE][:, c, off:512], E[(n - 1) % NE][:, c, off:512],
                                 E[n % NE][:, c, off:512], ALU.add, av_done[n - 1], exp_ready[(n, h)])

    def total(n):
        hg, qt, kt = steps[n]
        off = offset(n - 1)
        last = kt == 4 * qt + 3
        for j in range(4):
            k = p.mm(RS[32 * j:32 * j + 32, off:512], p.ones[:, :], E[(n - 1) % NE][:, j, off:512], kt == 1, last,
                     summed[n], rs_free[0], sig=j == 3)
        e_free[(n - 1) % NE] = e_free[n % NE] = k
        if last:
            q = slice(512 * qt, 512 * qt + 512)
            k = rs_free[0] = dve.do(lambda e: e.reciprocal(rec[:, :], RS), k, rec_free[0])
            rec_free[0] = p.tt(pool, avn[:, hg, q], avn[:, hg, q], rec[:, :], ALU.mult, k, copied[(hg, qt)])

    advance(24)
    restack(1)
    N = len(steps)
    for n in range(N + 3):
        rate = 5 if n < 24 else 4
        if n < N:
            hg, qt, kt = steps[n]
            while (hg, qt) not in biased:
                next(gen)
            score(n, 0)
        advance(1)
        if n < N:
            score(n, 1)
        advance(1)
        if 1 <= n <= N:
            weigh(n - 1)
        advance(1)
        if n >= 3 and n % 2:
            total(n - 2)
        advance(rate - 3)
        if n < N and kt == 15 and hg + 2 < 4:
            restack(hg + 2)


def outproj(p, b, pieces):
    pe, dve, act, pool = p.pe, p.dve, p.act, p.pool
    o = QS0 + 32768
    wh, wl = p.at([128, KC, D], F32R, o), p.at([128, KC, D], F32R, o + 8192)
    o += 16384
    ah = [p.at([128, KC, 512], F32R, o + 16384 * i) for i in range(2)]
    al = [p.at([128, KC, 512], F32R, o + 16384 * i + 8192) for i in range(2)]
    o += 32768
    xr = [p.at([128, 512], F32, o + 2048 * i) for i in range(8)]
    wraw = p.at([128, KC, D], F32, o + 16384)
    avn = p.qs[:, :, :, :].rearrange("p g a s -> p g (a s)").bitcast(F32)
    k = p.dma.go(wraw[:, :, :], p.a["L0_attn_Wo"].rearrange("(c p) n -> p c n", p=128))
    src = p.xa[S * b:S * (b + 1), :].rearrange("(n t p) d -> n t p d", t=4, p=128)
    dst = p.xc[S * b:S * (b + 1), :].rearrange("(n t p) d -> n t p d", t=4, p=128)
    kx, xr_free = {}, [None] * 8

    def load(n):
        kx[n] = p.dma.go(xr[n % 8][:, :], src[n // 4, n % 4], xr_free[n % 8])

    for n in range(8):
        load(n)
    loads = [p.dma.go(s, d) for s, d in pieces]
    k = p.af(wh[:, :, :], wraw[:, :, :], ACT.Copy, k)
    kw = p.tt(dve, wl[:, :, :], wraw[:, :, :], wh[:, :, :], ALU.subtract, k)
    a_free, ring_free = [None] * 2, [None] * 8
    ka = {}

    def split(q):
        i = q % 2
        x = avn[:, :, 512 * q:512 * q + 512]
        k = p.af(ah[i][:, :, :], x, ACT.Copy, a_free[i])
        ka[q] = p.tt(dve, al[i][:, :, :], x, ah[i][:, :, :], ALU.subtract, k)

    split(0)
    for q in range(4):
        i = q % 2
        if q < 3:
            split(q + 1)
        for tb in range(4):
            n = 4 * q + tb
            r, s = n % 8, n % 8
            c0 = slice(128 * tb, 128 * tb + 128)
            kb = p.tt(pool, xr[s][:, :], xr[s][:, :], p.bob[:, :], ALU.add, kx[n])
            for c in range(KC):
                p.mm(p.b[r], ah[i][:, c, c0], wh[:, c, :], c == 0, False, ring_free[r], ka[q], kw)
                p.mm(p.b[r], ah[i][:, c, c0], wl[:, c, :], False, False)
                k = p.mm(p.b[r], al[i][:, c, c0], wh[:, c, :], False, c == KC - 1, sig=c == KC - 1)
            ring_free[r] = p.tt(dve, xr[s][:, :], p.b[r], xr[s][:, :], ALU.add, k, kb)
            xr_free[s] = p.dma.go(dst[q, tb], xr[s][:, :], ring_free[r])
            if 4 <= n < 12:
                load(n + 4)
        a_free[i] = k
    return loads


def program(nc, a):
    p = Prog(nc, a)
    p.xa = nc.dram_tensor("xa", [T, D], F32).ap()
    p.xc = nc.dram_tensor("xc", [T, D], F32).ap()
    p.dga, p.dgb = (nc.dram_tensor(n, [IC, 128, 1024], F32).ap() for n in ("dga", "dgb"))
    p.dda, p.ddb = (nc.dram_tensor(n, [IC, 128, D], F32).ap() for n in ("dda", "ddb"))
    psum(p)
    constants(p)
    ffn_memory(p)
    ffn(p, a["L0_attn_X"].rearrange("b s d -> (b s) d"), p.xa, deq=Dequant(p))
    p.barrier()
    attention_vectors(p)
    p.barrier()
    p.qs = p.at([128, 4, 2, S], F16, QS0)
    p.ks = p.at([128, 4, 2, S], F16, C0)
    p.v = p.at([128, 16, D], F32, C0 + 32768)
    pieces = weight_pieces(p)
    for b in range(B):
        qkv(p, b)
        p.barrier()
        attention(p, b)
        p.barrier()
        gate_up = outproj(p, b, [x for row in pieces for x in row[0:2]] if b == B - 1 else [])
        p.barrier()
    kg, kd = {}, {}
    for i in range(IC):
        kg[i] = gate_up[2 * i:2 * i + 2]
        kd[i] = [p.dma.go(s, d) for s, d in pieces[i][2:4]]
    ffn(p, p.xc, a["out"].rearrange("b s d -> (b s) d"), loaded=(kg, kd))
    p.barrier()
    with nc.Block() as block:
        @block.sync
        def _(e):
            p.sp.run(e)

        @block.tensor
        def _(e):
            p.pe.run(e)

        @block.vector
        def _(e):
            p.dve.run(e)

        @block.scalar
        def _(e):
            p.act.run(e)

        @block.gpsimd
        def _(e):
            p.pool.run(e)


_INS = ["L0_attn_X", "L0_attn_ln_g", "L0_attn_ln_b", "L0_attn_Wq", "L0_attn_bq", "L0_attn_Wk", "L0_attn_bk",
        "L0_attn_Wv", "L0_attn_bv", "L0_attn_Wo", "L0_attn_bo", "L0_ffn_gate_up_packed", "L0_ffn_gate_up_scales",
        "L0_ffn_down_packed", "L0_ffn_down_scales"]


def kernel(**inputs):
    import numpy as np
    import concourse.bacc as bacc
    from concourse.bass_utils import run_bass_kernel_spmd

    nc = bacc.Bacc("TRN2", target_bir_lowering=False, num_devices=1)
    arrays, a = {}, {}
    for name in _INS:
        x = np.ascontiguousarray(inputs[name])
        arrays[name] = x
        a[name] = nc.dram_tensor(name, x.shape, mybir.dt.from_np(x.dtype), kind="ExternalInput").ap()
    a["out"] = nc.dram_tensor("out", (B, S, D), F32, kind="ExternalOutput").ap()
    program(nc, a)
    r = run_bass_kernel_spmd(nc, [arrays], core_ids=[0])
    return r.results[0]["out"]
```

```python
import concourse.bass as bass
import concourse.mybir as mybir

F32 = mybir.dt.float32
F32R = mybir.dt.float32r
F16 = mybir.dt.float16
BF16 = mybir.dt.bfloat16
I32 = mybir.dt.int32
U16 = mybir.dt.uint16
ALU = mybir.AluOpType
ACT = mybir.ActivationFunctionType
AX = mybir.AxisListType

B, S, D, H, DH = 2, 2048, 512, 16, 32
T = B * S
I = 1408
IC = I // 128
KC = D // 128
NT = T // 512
SC = float(1.0 / (32.0 ** 0.5))
NEG = -1.0e30
BASE = 16512
C0 = 7936
WD0 = C0 + 45056
A0 = C0 + 90112
X0 = A0 + 45056
H0 = X0 + 32768
XB0 = H0 + 20480
XR0 = XB0 + 8192
QS0 = A0
KP0 = C0 + 65536
LAG = 9


class Lane:

    def __init__(self, nc, name):
        self.nc, self.name = nc, name
        self.items, self.seen = [], {}
        self.phase = 0
        self.fresh()

    def fresh(self):
        self.sem = self.nc.alloc_semaphore(f"{self.name}{self.phase}")
        self.key = f"{self.name}{self.phase}"
        self.phase += 1
        self.n = 0

    def need(self, *toks):
        for t in toks:
            if t is None:
                continue
            key, sem, value = t
            if self.seen.get(key, 0) >= value:
                continue
            self.seen[key] = value
            self.items.append(lambda e, sem=sem, value=value: e.wait_ge(sem, value))

    def do(self, fn, *toks, sig=True):
        self.need(*toks)
        if not sig:
            self.items.append(fn)
            return None
        self.n += 1
        sem = self.sem
        self.items.append(lambda e: fn(e).then_inc(sem, 1))
        return (self.key, sem, self.n)

    def last(self):
        return (self.key, self.sem, self.n) if self.n else None

    def run(self, e):
        for f in self.items:
            f(e)


class Dma:

    N = 32

    def __init__(self, nc, sp):
        self.sp = sp
        self.sems = [nc.alloc_semaphore(f"dma{i}") for i in range(self.N)]
        self.count = [0] * self.N
        self.i = 0

    def go(self, dst, src, *toks):
        k = self.i % self.N
        self.i += 1
        sem = self.sems[k]
        if self.count[k]:
            self.sp.need((f"dma{k}", sem, self.count[k]))
        self.count[k] += 16
        self.sp.need(*toks)
        self.sp.items.append(lambda e: e.dma_start(dst, src).then_inc(sem, 16))
        return (f"dma{k}", sem, self.count[k])


class Prog:
    def __init__(self, nc, a):
        self.nc, self.a = nc, a
        self.pe, self.dve, self.act = Lane(nc, "pe"), Lane(nc, "dve"), Lane(nc, "act")
        self.pool, self.sp = Lane(nc, "pool"), Lane(nc, "sp")
        self.lanes = [self.pe, self.dve, self.act, self.pool, self.sp]
        self.dma = Dma(nc, self.sp)
        self.nuid = 0

    def at(self, shape, dt, off):
        self.nuid += 1
        return self.nc.alloc_sbuf_tensor_at(f"sb{self.nuid}", list(shape), dt, offset=BASE + off)

    def meet(self, skip, pe):
        count = list(self.dma.count)
        for key, _, value in skip:
            k = int(key[3:])
            count[k] = min(count[k], value - 16)
        toks = [ln.last() for ln in self.lanes]
        toks += [(f"dma{k}", self.dma.sems[k], c) for k, c in enumerate(count) if c > 0]
        for ln in self.lanes:
            ln.need(*(toks if pe is None or ln is not self.pe else pe))
        for ln in self.lanes:
            ln.fresh()

    def mm(self, out, l, r, st, sp, *toks, sig=False):
        return self.pe.do(lambda e: e.matmul(out, l, r, start=st, stop=sp), *toks, sig=sig)

    def tr(self, out, x, ident, *toks, sig=False):
        return self.pe.do(lambda e: e.transpose(out, x, ident), *toks, sig=sig)

    def af(self, out, x, func, *toks, **kw):
        return self.act.do(lambda e: e.activation(out, x, func, **kw), *toks)

    def tt(self, ln, out, x, y, op, *toks):
        return ln.do(lambda e: e.tensor_tensor(out, x, y, op), *toks)

    def ts(self, ln, out, x, s1, s2, op0, op1, *toks):
        if op1 is None:
            return ln.do(lambda e: e.tensor_scalar(out, x, s1, None, op0), *toks)
        return ln.do(lambda e: e.tensor_scalar(out, x, s1, s2, op0, op1), *toks)

    def stt(self, out, x, s, y, op0, op1, *toks):
        return self.dve.do(lambda e: e.scalar_tensor_tensor(out, x, s, y, op0, op1), *toks)

    def cp(self, ln, out, x, *toks):
        return ln.do(lambda e: e.tensor_copy(out, x), *toks)

    def rsqrt_steps(self, out, x, scale, eps, mult, w, *toks):
        v, g, t = w[:, 0, :], w[:, 1, :], w[:, 2, :]
        d = self.dve
        k = self.ts(d, v, x, scale / mult ** 2, eps / mult ** 2, ALU.mult, ALU.add, *toks)
        yield k
        k = self.ts(d, t.bitcast(I32), v.bitcast(I32), 1, None, ALU.logical_shift_right, None, k)
        yield k
        k = self.ts(d, g.bitcast(I32), t.bitcast(I32), -1.0, float(0x5F3759DF), ALU.mult, ALU.add, k)
        yield k
        for n in range(3):
            k = self.tt(d, t, g, g, ALU.mult, k)
            yield k
            k = self.stt(t, t, -0.5, v, ALU.mult, ALU.mult, k)
            yield k
            k = self.stt(out if n == 2 else g, t, 1.5, g, ALU.add, ALU.mult, k)
            yield k

    def rsqrt(self, *args):
        return list(self.rsqrt_steps(*args))[-1]


def constants(p):
    o = 0

    def take(shape, dt, size):
        nonlocal o
        t = p.at(shape, dt, o)
        o += (size + 31) // 32 * 32
        return t

    p.idf = take([128, 128], F32, 512)
    p.idh = take([128, 128], F16, 256)
    p.idb = take([128, 128], BF16, 256)
    p.mS = take([128, 128], BF16, 256)
    p.mT = take([128, 128], BF16, 256)
    p.ones = take([128, 32], F32, 128)
    p.two14 = take([128, 4], F32, 16)
    p.st = take([128, 4, 6], F32, 96)
    p.mv = take([128, 4, 2], F32, 32)
    p.rs = take([128, 4], F32, 32)
    p.w4 = take([128, 3, 4], F32, 48)
    p.ss = take([128, 4], F32, 32)
    p.r4 = take([128, 4], F32, 32)
    p.w5 = take([128, 3, 4], F32, 48)
    p.st2 = take([128, 4, 6], F32, 96)
    p.mv2 = take([128, 4, 2], F32, 32)
    p.rs2 = take([128, 4], F32, 32)
    p.bias = take([128, 4, 4], F32, 64)
    p.bvb = take([128, 512], F32, 2048)
    p.bob = take([128, 512], F32, 2048)
    p.sg = take([128, 22, 4], F32, 352)
    p.sd = take([128, 4, 11], F32, 176)
    p.junk = take([128, 512], BF16, 1024)
    assert o <= C0
    a, pool = p.a, p.pool
    k0 = pool.do(lambda e: e.memset(p.idf[:, :], 0.0))
    k1 = pool.do(lambda e: e.memset(p.mS[:, :], 0.0))
    k2 = pool.do(lambda e: e.memset(p.mT[:, :], 0.0))
    pool.do(lambda e: e.memset(p.ones[:, :], 1.0))
    pool.do(lambda e: e.memset(p.two14[:, :], 16384.0))
    p.kid = pool.do(lambda e: e.affine_select(out=p.idf[:, :], in_=p.idf[:, :], compare_op=ALU.not_equal, fill=1.0,
                                              base=0, pattern=[[-1, 128]], channel_multiplier=1), k0)
    pool.do(lambda e: e.affine_select(out=p.mS[:, :], in_=p.mS[:, :], compare_op=ALU.is_ge, fill=NEG,
                                      base=0, pattern=[[-1, 128]], channel_multiplier=1), k1)
    pool.do(lambda e: e.affine_select(out=p.mT[:, :], in_=p.mT[:, :], compare_op=ALU.is_ge, fill=NEG,
                                      base=0, pattern=[[1, 128]], channel_multiplier=-1), k2)
    p.cp(pool, p.idh[:, :], p.idf[:, :], p.kid)
    p.cp(pool, p.idb[:, :], p.idf[:, :], p.kid)
    p.marks = p.at([32, 4, 512], F16, H0)
    p.kmarks = pool.do(lambda e: e.memset(p.marks[:, :, :], 0.0))
    for s in range(2):
        p.kmarks = pool.do(lambda e, s=s: e.affine_select(
            out=p.marks[:, :, :], in_=p.marks[:, :, :], compare_op=ALU.not_equal, fill=1.0, base=-4 * s,
            pattern=[[-1, 4], [0, 512]], channel_multiplier=1), p.kmarks)


def attention_vectors(p):
    a = p.a
    rows = p.at([16, 128], F32, XR0 + 7168)
    ks = [p.dma.go(rows[4 * n:4 * n + 4, :], a[f"L0_attn_{name}"].rearrange("(c p) -> c p", p=128))
          for n, name in enumerate(("ln_g", "ln_b", "bq", "bk"))]
    p.dma.go(p.bvb[:, :], a["L0_attn_bv"].partition_broadcast(128))
    p.dma.go(p.bob[:, :], a["L0_attn_bo"].partition_broadcast(128))
    p.kdk = [p.dma.go(p.dk.rearrange("p (j r s) -> p j r s", j=4, r=4)[:, :, r, :], p.marks[:, :, :], p.kmarks)
             for r in range(4)]

    def turn():
        k = p.tr(p.b[7][:, 0:16], rows[:, :], p.idf[0:16, 0:16], *ks, sig=True)
        k = p.cp(p.dve, p.bias[:, :, :].rearrange("p a b -> p (a b)"), p.b[7][:, 0:16], k)
        return p.ts(p.dve, p.bias[:, 2, :], p.bias[:, 2, :], SC, None, ALU.mult, None, k)
    return turn


def psum(p):
    p.bank = [p.nc.alloc_psum_tensor(f"ps{i}", [128, 512], F32) for i in range(2)]
    p.pair = [p.nc.alloc_psum_tensor(f"pp{i}", [128, 2, 512], F32) for i in range(3)]
    p.b = [p.bank[0][:, :], p.bank[1][:, :]] + [p.pair[i][:, n, :] for i in range(3) for n in range(2)]


def ffn_memory(p):
    p.wg = p.at([128, IC, KC, 2, 128], F32R, C0)
    p.wd = p.at([128, IC, 2, D], F32R, WD0)
    p.x1 = [p.at([128, KC, 512], F32R, X0 + 16384 * i) for i in range(2)]
    p.x2 = [p.at([128, KC, 512], F32R, X0 + 16384 * i + 8192) for i in range(2)]
    p.acc = [[p.at([128, 512], F32, A0 + 6144 * u + 2048 * i) for i in range(3)] for u in range(2)]
    p.tmp = [p.at([128, 512], F32, A0 + 12288 + 2048 * i) for i in range(2)]
    p.ysb = [p.at([128, 512], F32, A0 + 16384 + 2048 * i) for i in range(4)]
    p.h1 = [p.at([128, 512], F32R, H0 + 2048 * i) for i in range(3)]
    p.h2 = [p.at([128, 512], F32R, H0 + 6144 + 2048 * i) for i in range(3)]
    p.sil = [p.at([128, 512], F32, H0 + 12288 + 2048 * i) for i in range(2)]
    p.h = [p.at([128, 512], F32, H0 + 16384 + 2048 * i) for i in range(2)]
    p.xb = [p.at([128, 512], F32, XB0 + 2048 * i) for i in range(4)]
    p.xr = [p.at([128, 512], F32, XR0 + 2048 * i) for i in range(4)]


class Dequant:

    def __init__(self, p):
        self.p = p
        a, dve = p.a, p.dve
        o = X0 + 16384
        self.pk = p.at([128, IC, 192], I32, o)
        self.v = p.at([128, 4, 768], U16, o + 8448)
        self.w32 = [p.at([128, 4, 128], F32, XR0 + 2048 * i) for i in range(2)]
        self.t1 = [p.at([128, 384], U16, XR0 + 4096 + 1536 * i) for i in range(2)]
        sc16 = p.at([11, 2816 + 512], F16, A0 + 24576 + 13312)
        sc32 = p.at([11, 2816 + 512], F32, A0 + 24576)
        gu = a["L0_ffn_gate_up_packed"].rearrange("(u i p) w -> u p i w", u=2, p=128)
        ks1 = p.dma.go(sc16[0:4, 0:2816], a["L0_ffn_gate_up_scales"])
        ks2 = p.dma.go(sc16[0:11, 2816:3328], a["L0_ffn_down_scales"])
        self.kpk = [p.dma.go(self.pk[:, :, 64 * u:64 * u + 64], gu[u]) for u in range(2)]
        dn = a["L0_ffn_down_packed"].rearrange("(h p) (i w) -> h p i w", p=128, w=16)
        self.kpk += [p.dma.go(self.pk[:, :, 128 + 16 * h:144 + 16 * h], dn[h]) for h in range(4)]
        c1 = p.af(sc32[0:4, 0:2816], sc16[0:4, 0:2816], ACT.Copy, ks1)
        c2 = p.af(sc32[0:11, 2816:3328], sc16[0:11, 2816:3328], ACT.Copy, ks2, scale=16384.0)
        for t in range(22):
            k1 = p.tr(p.b[4][:, 4 * t:4 * t + 4], sc32[0:4, 128 * t:128 * t + 128], p.idf[0:4, 0:4], p.kid, c1,
                      sig=t == 21)
        for t in range(4):
            k2 = p.tr(p.b[5][:, 11 * t:11 * t + 11], sc32[0:11, 2816 + 128 * t:2944 + 128 * t], p.idf[0:11, 0:11], c2,
                      sig=t == 3)
        self.e1 = p.af(p.sg[:, :, :].rearrange("p a b -> p (a b)"), p.b[4][:, 0:88], ACT.Copy, k1)
        self.e2 = p.af(p.sd[:, :, :].rearrange("p a b -> p (a b)"), p.b[5][:, 0:44], ACT.Copy, k2)
        self.two14 = p.two14[:, :].unsqueeze(2).unsqueeze(3).broadcast_to([128, 4, 32, 4])
        self.t_free = [None, None]
        self.v_free = [None, None]
        self.w_free = [None, None]
        self.n = 0
        self.kd = {}

    def decode(self, i):
        p, dve = self.p, self.p.dve
        half = slice(384 * (i % 2), 384 * (i % 2) + 384)
        u = self.pk[:, :, :].rearrange("p a b -> p (a b)").bitcast(U16)[:, 384 * i:384 * i + 384]
        pend, done = [], None
        for m in range(5):
            if m < 4:
                t, v = self.t1[m % 2], self.v[:, m, half]
                p.ts(dve, t[:, :], u, 12 - 4 * m, 0x8000, ALU.logical_shift_left, ALU.bitwise_and, self.t_free[m % 2],
                     *self.kpk)
                yield
                sh = 9 - 4 * m
                op = ALU.logical_shift_left if sh >= 0 else ALU.logical_shift_right
                k = p.ts(dve, v, u, abs(sh), 0x0E00, op, ALU.bitwise_and, self.v_free[i % 2])
                pend.append((m, t, v, k))
                yield
            if m >= 1:
                j, t, v, k = pend.pop(0)
                done = self.t_free[j % 2] = p.tt(dve, v, v, t[:, :], ALU.bitwise_or, k)
                if m == 4:
                    self.kd[i] = (384 * (i % 2), done)
                yield

    def scaled(self, i, part):
        p = self.p
        at, k = self.kd[i]
        v = self.v[:, :, at + 128 * part:at + 128 * part + 128].bitcast(F16).rearrange("p b (g q) -> p g q b", g=4)
        s = self.two14 if part < 2 else p.sd[:, :, i].unsqueeze(2).unsqueeze(3).broadcast_to([128, 4, 32, 4])
        r = self.n % 2
        self.n += 1
        w = self.w32[r]
        k = p.tt(p.pool, w[:, :, :].rearrange("p g (q b) -> p g q b", b=4), v, s, ALU.mult, k, self.e2, p.kid,
                 self.w_free[r])
        self.v_free[i % 2] = k
        return r, k

    def turned(self, i, part, r, kw, bk, free):
        p = self.p
        for g in range(4):
            k = p.tr(bk[:, 128 * g:128 * g + 128], self.w32[r][:, g, :], p.idf[:, :], kw, free, sig=g == 3)
        self.w_free[r] = k
        if part < 2:
            return p.af(p.wg[:, i, :, part, :], bk.rearrange("p (g o) -> p g o", g=4), ACT.Copy, k)
        k = p.af(p.wd[:, i, 0, :], bk, ACT.Copy, k)
        return p.tt(p.dve, p.wd[:, i, 1, :], bk, p.wd[:, i, 0, :], ALU.subtract, k)


def weight_pieces(p):
    out = []
    for i in range(IC):
        row = [(p.wg[:, i, :, :, :].rearrange("p a b c -> p (a b c)").bitcast(F32), p.dg[i])]
        row += [(p.wd[:, i, :, :].rearrange("p a b -> p (a b)").bitcast(F32), p.dd[i])]
        out.append(row)
    return out


def ffn(p, src, dst, src_done, dst_done, dequantize=False, loaded=None, ahead=None, start=None, settle=()):
    pe, dve, act, pool = p.pe, p.dve, p.act, p.pool
    ring, Y = p.b[0:4], p.b[4:8]
    srcv = src.rearrange("(n t p) d -> n t p d", t=4, p=128)
    dstv = dst.rearrange("(n t p) d -> n t p d", t=4, p=128)
    pieces = weight_pieces(p)
    xb_free, x_free, x_ready, kx = [None] * 4, [None, None], {}, {}
    ring_free, nring = [None] * 4, [0]
    acc_free, tmp_free = [[None] * 3, [None] * 3], [None] * 2
    sil_free, h_free, hh_free, h_ready = [None] * 2, [None] * 2, [None] * 3, {}
    y_free, ysb_free, xr_free, kr = [None] * 4, [None] * 4, [None] * 4, {}
    last = {"mv": None, "r4": None, "turned": None}
    ky, later = [None] * 4, []

    def take():
        nring[0] += 1
        return (nring[0] - 1) % 4

    def load(tt):
        kx[tt] = [p.dma.go(p.xb[tb][:, :], srcv[tt, tb], xb_free[tb], src_done.get(4 * tt + tb)) for tb in range(4)]

    def stats(tt, kn):
        free, last["mv"] = last["mv"], kn
        return norm_steps(p, p.xb, kx[tt], kn, (p.st, p.mv, p.rs, p.w4), free and free[3])

    def chunk(tt, c, kn):
        r = take()
        for tb in range(4):
            k = p.tr(ring[r][:, 128 * tb:128 * tb + 128], p.xb[tb][:, 128 * c:128 * c + 128], p.idf[:, :], kn[tb],
                     ring_free[r], sig=tb == 3)
        if c == 3:
            xb_free[:] = [k] * 4
        i = tt % 2
        ka = p.af(p.x1[i][:, c, :], ring[r], ACT.Copy, k, x_free[i])
        ring_free[r] = x_ready[(tt, c)] = p.tt(dve, p.x2[i][:, c, :], ring[r], p.x1[i][:, c, :], ALU.subtract, ka)

    def scale(m):
        if m < 3 * IC:
            todo[m] = deq.scaled(*divmod(m, 3))

    def turned(m):
        i, part = divmod(m, 3)
        w, k = todo.pop(m)
        r = take()
        k = ring_free[r] = last["turned"] = deq.turned(i, part, w, k, ring[r], ring_free[r])
        (kg if part < 2 else kdn).setdefault(i, []).append(k)
        scale(m + 2)

    def group(tt, i, c, u):
        n, r = tt * IC + i, take()
        w, a = p.wg[:, i, c, u, :], p.acc[u][n % 3][:, :]
        p.mm(ring[r], w, p.x1[tt % 2][:, c, :], True, False, ring_free[r], x_ready[(tt, c)], *kg[i])
        k = p.mm(ring[r], w, p.x2[tt % 2][:, c, :], False, True, sig=True)
        if i == IC - 1 and c == KC - 1:
            x_free[tt % 2] = k
        return lambda: evacuate(n, c, u, r, a, p.sg[:, IC * u + i, c:c + 1], k)

    def evacuate(n, c, u, r, a, s, k):
        if c == 0:
            ring_free[r] = acc_k[u] = p.af(a, ring[r], ACT.Copy, k, ksg, acc_free[u][n % 3], scale=s)
        elif c == 1 and u == 1:
            t = p.tmp[n % 2][:, :]
            ring_free[r] = k = p.af(t, ring[r], ACT.Copy, k, tmp_free[n % 2], scale=s)
            acc_k[u] = tmp_free[n % 2] = p.tt(pool, a, a, t, ALU.add, k, acc_k[u])
        else:
            ring_free[r] = acc_k[u] = p.stt(a, ring[r], s, a, ALU.mult, ALU.add, k, ksg, acc_k[u])

    def gated(tt, i):
        n = tt * IC + i
        s, h = p.sil[n % 2], p.h[n % 2]
        k = acc_free[0][n % 3] = p.af(s[:, :], p.acc[0][n % 3][:, :], ACT.Silu, acc_k[0], sil_free[n % 2])
        ln = dve if deq is not None and tt == 0 else pool
        h_ready[n] = sil_free[n % 2] = acc_free[1][n % 3] = p.tt(ln, h[:, :], s[:, :], p.acc[1][n % 3][:, :], ALU.mult,
                                                                 k, acc_k[1], h_free[n % 2])

    def parts(n):
        h, h1 = p.h[n % 2], p.h1[n % 3]
        k1 = p.af(h1[:, :], h[:, :], ACT.Copy, h_ready[n], hh_free[n % 3])
        return lambda: rest(n, k1)

    def rest(n, k1):
        h, h1, h2 = p.h[n % 2], p.h1[n % 3], p.h2[n % 3]
        h_free[n % 2] = h_ready[n] = p.tt(pool, h2[:, :], h[:, :], h1[:, :], ALU.subtract, k1)

    def down(n, tb):
        tt, i = divmod(n, IC)
        h1, h2 = p.h1[n % 3], p.h2[n % 3]
        c = slice(128 * tb, 128 * tb + 128)
        end = i == IC - 1
        p.mm(Y[tb], h1[:, c], p.wd[:, i, 0, :], i == 0, False, h_ready[n], y_free[tb], *kdn[i])
        p.mm(Y[tb], h1[:, c], p.wd[:, i, 1, :], False, False)
        k = p.mm(Y[tb], h2[:, c], p.wd[:, i, 0, :], False, end, sig=end or tb == 3)
        if tb == 3:
            hh_free[n % 3] = k
        if end:
            y = p.ysb[tb][:, :]
            k = y_free[tb] = p.af(y, Y[tb], ACT.Copy, k, ysb_free[tb])
            ky[tb] = k
            if tb == 3:
                later.append(finish(tt))

    def residual(tt):
        kr[tt] = [p.dma.go(p.xr[tb][:, :], srcv[tt, tb], xr_free[tb], src_done.get(4 * tt + tb)) for tb in range(4)]

    def finish(tt):
        ks = []
        for tb in range(4):
            o, y = p.ss[:, tb:tb + 1], p.ysb[tb][:, :]
            ks.append(p.af(p.junk[:, :], y, ACT.Square, ky[tb], last["r4"], act.last(), accum_out=o))
            yield from range(1, 4)
        for k in p.rsqrt_steps(p.r4[:, :], p.ss[:, :], 1.0 / D, 1e-6, 0.5, p.w5, *ks):
            yield
        for tb in range(4):
            x = p.xr[tb][:, :]
            ko = p.stt(x, p.ysb[tb][:, :], p.r4[:, tb:tb + 1], x, ALU.mult, ALU.add, kr[tt][tb], k)
            ysb_free[tb] = last["r4"] = ko
            xr_free[tb] = dst_done[4 * tt + tb] = p.dma.go(dstv[tt, tb], x, ko)
            yield

    def tick():
        if later and next(later[0], 0) == 0:
            later.pop(0)
            tick()

    todo, acc_k = {}, [None, None]
    if start is None:
        load(0)
    deq = Dequant(p) if dequantize else None
    vectors = attention_vectors(p) if dequantize else None
    kg, kdn = loaded or ({}, {})
    ksg = deq.e1 if dequantize else None
    kn = []
    if start is None:
        for _ in stats(0, kn):
            pass
    else:
        last["mv"] = kn = start["kn"]
    if deq is not None:
        for i in range(2):
            for _ in deq.decode(i):
                pass
            if i == 0:
                scale(0)
                scale(1)
    for c in range(KC):
        chunk(0, c, kn)
    load(1)
    if deq is not None:
        for m in range(3):
            turned(m)
        y_free[3] = vectors()
        act.need(*p.kdk)
    for tt in range(NT):
        first = deq is not None and tt == 0
        delay = 2 if start is not None and tt == 0 else 0
        for i in range(IC):
            n = tt * IC + i
            turn = first and i + 1 < IC
            for c in range(KC):
                ready = [group(tt, i, c, u) for u in (1, 0)]
                if c:
                    ready.reverse()
                for f in ready:
                    f()
                    tick()
                    if tt == NT - 1 and i > 5:
                        tick()
                if c == 0 and n:
                    subtract = parts(n - 1)
                if c == 1 and n:
                    subtract()
                if 4 * n + c >= LAG:
                    down(*divmod(4 * n + c - LAG, 4))
                if turn and c < 3:
                    turned(3 * (i + 1) + c)
                if first and c == 0:
                    decoding = deq.decode(i + 3) if i + 3 < IC else iter(())
                    if i == 0:
                        for _ in deq.decode(2):
                            pass
                if first and c:
                    for _ in range(5):
                        next(decoding, None)
                if tt + 1 < NT:
                    if c == 1 and 0 <= i - delay - 4 < 4 and not first:
                        chunk(tt + 1, i - delay - 4, kn)
                    if i == IC - 1 and first:
                        x_free[1] = last["turned"]
                        chunk(tt + 1, c, kn)
            if n == 0:
                for ln in (act, dve, pool):
                    ln.need(*settle[:12])
                p.sp.need(*settle)
            gated(tt, i)
            if i == (5 if first else delay) and tt + 1 < NT:
                kn = []
                later.append(stats(tt + 1, kn))
            if i == (IC - 1 if first else 8 + delay):
                if first:
                    xr_free[:] = [last["turned"]] * 4
                residual(tt)
                if tt + 2 < NT:
                    load(tt + 2)
            if tt == NT - 1 and i == 3 and ahead is not None:
                later.append(ahead(last["mv"][3], *xb_free))
            if deq is not None and tt in (2, 3) and i >= 3:
                for s, d in pieces[i - 3 + 8 * (tt - 2)] if i - 3 + 8 * (tt - 2) < IC else ():
                    p.dma.go(d, s)
    n = NT * IC
    parts(n - 1)()
    for d in range(4 * n - LAG, 4 * n):
        down(*divmod(d, 4))
    while later:
        tick()
    return xr_free, ring_free + y_free


def norm_steps(p, xb, kx, kn, bufs, free):
    st, mv, rs, w = bufs
    dve, ks = p.dve, []
    for tb in range(4):
        o, x, m = st[:, tb, :], xb[tb][:, :], mv[:, tb, :]
        k = dve.do(lambda e, o=o, x=x: e.bn_stats(o, x), kx[tb])
        yield
        ks.append(dve.do(lambda e, o=o, m=m: e.bn_aggr(m, o), k, free))
        yield
    for k in p.rsqrt_steps(rs[:, :], mv[:, :, 1], 1.0, 1e-5, 1.0, w, *ks):
        yield
    for tb in range(4):
        kn.append(p.ts(dve, xb[tb][:, :], xb[tb][:, :], mv[:, tb, 0:1], rs[:, tb:tb + 1], ALU.subtract, ALU.mult, k))
        yield


class Qkv:

    def __init__(self, p, b, raw):
        self.p, self.b = p, b
        self.wraw = [p.at([128, KC, D], F32, o) for o in raw]
        self.srcv = p.xa[S * b:S * (b + 1), :].rearrange("(n t p) d -> n t p d", t=4, p=128)
        self.xb = p.xb
        self.bufs = [(p.st, p.mv, p.rs, p.w4), (p.st2, p.mv2, p.rs2, p.w5)]
        self.s_free, self.xb_free = [None, None], [None] * 4
        self.kx, self.kraw = {}, {}

    def load(self, tt, *toks):
        p = self.p
        self.kx[tt] = [p.dma.go(self.xb[tb][:, :], self.srcv[tt, tb], self.xb_free[tb],
                                p.xa_done[16 * self.b + 4 * tt + tb], *toks) for tb in range(4)]

    def weight(self, n, *toks):
        self.kraw[n] = self.p.dma.go(self.wraw[n][:, :, :], self.p.a["L0_attn_" + ("Wq", "Wk", "Wv")[n]].rearrange(
            "(c p) n -> p c n", p=128), *toks)

    def norm(self, tt):
        for rnd in range(2):
            kn = []
            yield from norm_steps(self.p, self.xb, self.kx[tt], kn, self.bufs[rnd], self.s_free[rnd])
            self.kx[tt], self.s_free[rnd] = kn, kn[3]

    def run(self, x1_free):
        p = self.p
        pe, dve, act, pool = p.pe, p.dve, p.act, p.pool
        o = QS0 + 32768
        wh = [p.at([128, KC, D], F32R, o + 16384 * i) for i in range(3)]
        wl = [p.at([128, KC, D], F32R, o + 16384 * i + 8192) for i in range(3)]
        xnt = [p.at([128, 512], F32, KP0 + 16384 + 2048 * i) for i in range(2)]
        q32 = [p.at([128, 512], F32, KP0 + 20480 + 2048 * i) for i in range(2)]
        xo = [KP0, o + 49152]
        xh = [p.at([128, KC, 512], F32R, xo[i]) for i in range(2)]
        xl = [p.at([128, KC, 512], F32R, xo[i] + 8192) for i in range(2)]
        tbank, t_free = [p.b[0], p.b[1]], [None, None]
        ring, ring_free, nr = p.b[2:8], [None] * 6, [0]
        xnt_free, q32_free, x_free = [None] * 2, [None] * 2, [[], list(x1_free)]
        x_ready, kw, nq = {}, {}, [0]
        kx, xb = self.kx, self.xb

        def turn(tt, c):
            i, f = tt % 2, c % 2
            for tb in range(4):
                k = p.tr(tbank[f][:, 128 * tb:128 * tb + 128], xb[tb][:, 128 * c:128 * c + 128], p.idf[:, :],
                         kx[tt][tb], t_free[f], sig=tb == 3)
            ka = t_free[f] = p.af(xnt[f][:, :], tbank[f], ACT.Identity, k, xnt_free[f], scale=p.bias[:, 0, c:c + 1],
                                  bias=p.bias[:, 1, c:c + 1])
            kh = p.cp(dve, xh[i][:, c, :], xnt[f][:, :], ka, *x_free[i])
            xnt_free[f] = x_ready[(tt, c)] = p.tt(dve, xl[i][:, c, :], xnt[f][:, :], xh[i][:, c, :], ALU.subtract, kh)
            if c == 3:
                self.xb_free = [k] * 4

        def split(n, *toks):
            ka = p.af(wh[n][:, :, :], self.wraw[n][:, :, :], ACT.Copy, self.kraw[n], *toks)
            kw[n] = p.tt(dve, wl[n][:, :, :], self.wraw[n][:, :, :], wh[n][:, :, :], ALU.subtract, ka)

        def group(tt, lh, ll, rh, rl, k, beside=None):
            r = nr[0] % 6
            nr[0] += 1
            for c in range(KC):
                p.mm(ring[r], lh(c), rh(c), c == 0, False, ring_free[r], x_ready[(tt, c)], k)
                p.mm(ring[r], lh(c), rl(c), False, False)
                k = p.mm(ring[r], ll(c), rh(c), False, c == KC - 1, sig=c == KC - 1)
                if beside is not None:
                    beside()
            return r, k

        def features(tt, f, n):
            i = tt % 2
            ts_, fs = slice(512 * tt, 512 * tt + 512), slice(128 * f, 128 * f + 128)
            dst = (p.qs, p.ks)[n]
            r, k = group(tt, lambda c: wh[n][:, c, fs], lambda c: wl[n][:, c, fs], lambda c: xh[i][:, c, :],
                         lambda c: xl[i][:, c, :], kw[n])
            s = nq[0] % 2
            nq[0] += 1
            ka = ring_free[r] = p.af(q32[s][:, :], ring[r], ACT.Identity, k, q32_free[s], scale=SC if n == 0 else 1.0,
                                     bias=p.bias[:, 2 + n, f:f + 1])
            kh = p.cp(dve, dst[:, f, 0, ts_], q32[s][:, :], ka)
            q32_free[s] = p.tt(pool, dst[:, f, 1, ts_], q32[s][:, :], dst[:, f, 0, ts_], ALU.subtract, kh)

        def values(tt, tb, beside=None):
            i = tt % 2
            c0 = slice(128 * tb, 128 * tb + 128)
            r, k = group(tt, lambda c: xh[i][:, c, c0], lambda c: xl[i][:, c, c0], lambda c: wh[2][:, c, :],
                         lambda c: wl[2][:, c, :], kw[2], beside)
            ring_free[r] = p.tt(dve, p.v[:, 4 * tt + tb, :], ring[r], p.bvb[:, :], ALU.add, k)
            if tb == 3:
                x_free[i] = [k]

        turn(0, 0)
        turn(0, 1)
        split(1)
        turn(0, 2)
        turn(0, 3)
        split(0, kw[1])
        split(2, *x1_free[:8])
        self.load(1)
        later, rest = [], []
        for tt in range(4):
            if tt < 3:
                later.append(self.norm(tt + 1))
            for g in range(8):
                if tt == 3 and g == 2:
                    att = Attention(p, self.b, [pe.last(), dve.last(), pool.last()])
                features(tt, g // 2, 1 - g % 2)
                for _ in range(7):
                    if later and next(later[0], 0) == 0:
                        later.pop(0)
            for tb in range(4):
                if tt == 3:
                    rest.append(lambda beside, tb=tb: values(3, tb, beside))
                else:
                    values(tt, tb)
                    turn(tt + 1, tb)
            if tt < 2:
                self.load(tt + 2)
        return att, rest, ring_free


class Attention:
    def __init__(self, p, b, ready):
        self.p, self.b = p, b
        o = QS0 + 32768
        self.kp = [p.at([128, 4, S], F16, KP0), p.at([128, 4, S], F16, o)]
        self.qp = [p.at([128, 4, S], F16, o + 65536 - 49152 * i) for i in range(2)]
        self.stacked, self.last_use, self.kc = {}, {}, {}
        self.restack(0, *ready)
        self.marks(0, *ready)

    def restack(self, hg, *toks):
        p, i = self.p, hg % 2
        for j in range(4):
            rows, ks = slice(32 * j, 32 * j + 32), []
            for r, (wk, wq) in enumerate(((0, 0), (1, 0), (0, 1))):
                at = slice(32 * r, 32 * r + 32)
                ks.append(p.dma.go(self.kp[i][at, j, :], p.ks[rows, hg, wk, :], self.last_use.get(hg - 2), *toks))
                ks.append(p.dma.go(self.qp[i][at, j, :], p.qs[rows, hg, wq, :], self.last_use.get(hg - 2), *toks))
            self.stacked[(hg, j)] = ks

    def marks(self, i, *toks):
        self.kc[i] = self.p.dma.go(self.kp[i][96:128, :, :].rearrange("p j s -> p (j s)"), self.p.dk, *self.p.kdk, *toks)

    def pending(self):
        return [t for ks in self.stacked.values() for t in ks] + list(self.kc.values())

    def run(self, out, before, banks):
        p = self.p
        pe, dve, act, pool = p.pe, p.dve, p.act, p.pool
        kp, qp = self.kp, self.qp
        o = QS0 + 65536
        NE = 4
        E = [p.at([128, 4, 512], F32, o + 8192 * i) for i in range(NE)]
        o = KP0 + 16384
        rec = p.at([128, 512], F32, o)
        pm = [p.at([128, 16, 4], F32, o + 2048 + 256 * i) for i in range(2)]
        nm = [p.at([128, 4, 4], F32, o + 2560 + 64 * i) for i in range(2)]
        mc = [p.at([128, 4, 32], F16, o + 2688 + 256 * i) for i in range(2)]
        mbank = [p.b[0], p.b[1]]
        st = p.b[3:6]
        AV, RS = p.b[6], p.b[7]
        avn = p.qs[:, :, :, :].rearrange("p g a s -> p g (a s)").bitcast(F32)

        mc_free = [act.do(lambda e, x=mc[i]: e.activation(x[:, :, :], p.mS[:, :].rearrange("p (a b) -> p a b", a=4),
                                                          ACT.Copy, scale=0.0)) for i in range(2)]

        m_free, nmx = [None, None], [0]
        pm_free, nm_free, ngrp = [None, None], [None, None], [0]
        biased = {}

        def take():
            nmx[0] = (nmx[0] + 1) % len(mbank)
            return nmx[0]

        def max_units():
            pend = None
            for hg in range(4):
                i = hg % 2
                for qt in range(4):
                    g = ngrp[0] % 2
                    ngrp[0] += 1
                    cnt = 0
                    for qb in range(4):
                        q0 = 512 * qt + 128 * qb
                        nk = q0 + 128
                        nj = (4, 2, 1, 1)[qb]
                        units = [(j, 1, ck) for j in range(4) for ck in range(qt)]
                        units += [(j, nj, qt) for j in range(0, 4, nj)]
                        for j0, many, ck in sorted(units):
                            k0, k1 = 512 * ck, min(512 * ck + 512, nk)
                            r, w = take(), k1 - k0
                            diag = ck == qt
                            for j in range(j0, j0 + many):
                                c0 = w * (j - j0)
                                k = p.mm(mbank[r][:, c0:c0 + w], qp[i][0:96, j, q0:q0 + 128], kp[i][0:96, j, k0:k1],
                                         True, not diag, m_free[r], *self.stacked[(hg, j)], sig=not diag)
                                if diag:
                                    k = p.mm(mbank[r][:, c0 + w - 128:c0 + w], p.idb[:, :], p.mS[:, :], False, True,
                                             sig=j == j0 + many - 1)
                            out = pm[g][:, 4 * qb + j0:4 * qb + j0 + many, ck]
                            x = mbank[r][:, 0:many * w].rearrange("p (j k) -> p j k", j=many)
                            m_free[r] = dve.do(lambda e, out=out, x=x: e.reduce_max(out, x, AX.X), k, pm_free[g])
                            cnt += 1
                            spent[0] += many * w + 64
                            if pend is not None and cnt == 4:
                                pend()
                                pend = None
                            yield 1
                    pend = combine(hg, qt, g)
            pend()
            yield 1

        def combine(hg, qt, g):
            out, x = nm[g][:, :, :].rearrange("p a b -> p (a b)"), pm[g][:, :, 0:qt + 1]
            k = dve.do(lambda e: e.reduce_max(out, x, AX.X, negate=True), dve.last(), nm_free[g])
            pm_free[g] = k
            k = p.cp(dve, mc[g][:, :, 0:4], nm[g][:, :, :], k, mc_free[g])
            kd = nm_free[g] = p.tt(dve, mc[g][:, :, 4:8], nm[g][:, :, :], mc[g][:, :, 0:4], ALU.subtract, k)

            def rows():
                r = take()
                for qb in range(4):
                    k = p.mm(mbank[r][96:128, 128 * qb:128 * qb + 128], mc[g][:, qb, :], p.idh[:, :], True, True, kd,
                             m_free[r], sig=qb == 3)
                mc_free[g] = k
                q = slice(512 * qt, 512 * qt + 512)
                i = hg % 2
                k = m_free[r] = p.af(qp[i][96:128, 0, q], mbank[r][96:128, :], ACT.Copy, k, self.last_use.get(hg - 2))
                biased[(hg, qt)] = [k] + [p.dma.go(qp[i][96:128, j, q], qp[i][96:128, 0, q], k) for j in range(1, 4)]
            return rows

        gen = max_units()
        spent, work, parts = [0], [0], []

        def advance(w):
            work[0] += w
            if parts:
                parts.pop(0)()
                spent[0] += 450
            while spent[0] < min(9000 + work[0] * PACE * 3, 40000 + work[0] * PACE) and next(gen, 0) != 0:
                pass

        steps = [(hg, qt, kt) for hg in range(4) for qt in range(4) for kt in range(4 * qt + 4)]
        st_free, nst = [None] * 3, [0]
        e_free, exp_ready, av_done, summed = [None] * NE, {}, {}, {}
        av_free, rs_free, rec_free = [None], [None], [None]
        copied, normed = {}, {}

        def offset(n):
            hg, qt, kt = steps[n]
            return max(0, kt - 4 * qt) * 128

        def score(n, j):
            hg, qt, kt = steps[n]
            i, off = hg % 2, offset(n)
            diag = kt >= 4 * qt
            r = nst[0] = (nst[0] + 1) % 3
            k = p.mm(st[r][:, off:512], kp[i][:, j, 128 * kt:128 * kt + 128], qp[i][:, j, 512 * qt + off:512 * qt + 512],
                     True, not diag, st_free[r], self.kc[i], *biased[(hg, qt)], sig=not diag)
            if diag:
                k = p.mm(st[r][:, off:off + 128], p.idb[:, :], p.mT[:, :], False, True, sig=True)
            st_free[r] = exp_ready[(n, j)] = p.af(E[n % NE][:, j, off:512], st[r][:, off:512], ACT.Exp, k,
                                                  e_free[n % NE])
            self.last_use[hg] = k

        def weigh(n):
            hg, qt, kt = steps[n]
            off = offset(n)
            for j in range(4):
                h = 4 * hg + j
                k = p.mm(AV[32 * j:32 * j + 32, off:512], p.v[:, kt, 32 * h:32 * h + 32], E[n % NE][:, j, off:512], kt == 0,
                         kt == 4 * qt + 3, exp_ready[(n, j)], av_free[0], sig=j == 3)
            av_done[n] = k
            if kt == 4 * qt + 3:
                q = slice(512 * qt, 512 * qt + 512)
                av_free[0] = copied[(hg, qt)] = p.af(avn[:, hg, q], AV, ACT.Copy, k)
            if n % 2:
                for h in range(2):
                    c = slice(2 * h, 2 * h + 2)
                    summed[n] = p.tt(pool, E[(n - 1) % NE][:, c, off:512], E[(n - 1) % NE][:, c, off:512],
                                     E[n % NE][:, c, off:512], ALU.add, av_done[n - 1], exp_ready[(n, 2 * h + 1)])

        def total(n):
            hg, qt, kt = steps[n]
            off = offset(n - 1)
            last = kt == 4 * qt + 3
            for j in range(4):
                k = p.mm(RS[32 * j:32 * j + 32, off:512], p.ones[:, :], E[(n - 1) % NE][:, j, off:512], kt == 1, last,
                         summed[n], rs_free[0], sig=j == 3)
            e_free[(n - 1) % NE] = e_free[n % NE] = k
            if last:
                q = slice(512 * qt, 512 * qt + 512)

                def invert(c, k=k):
                    x = slice(64 * c, 64 * c + 64)
                    rs_free[0] = k = dve.do(lambda e: e.reciprocal(rec[:, x], RS[:, x]), k, rec_free[0])
                    if c == 7:
                        rec_free[0] = normed[(hg, qt)] = p.tt(pool, avn[:, hg, q], avn[:, hg, q], rec[:, :], ALU.mult, k,
                                                              copied[(hg, qt)])
                parts.extend(lambda c=c: invert(c) for c in range(8))

        total_work = sum((512 - offset(n)) * 10 for n in range(len(steps)))
        total_max = sum(4 * (512 * qt + 128 * qb + 128) + 64 * (4 * qt + (1, 2, 4, 4)[qb])
                        for qt in range(4) for qb in range(4)) * 4 + 16 * 8 * 450
        PACE = total_max / total_work
        for f in before:
            f(lambda: next(gen))
        p.af(p.junk[:, 0:1], p.ones[:, 0:1], ACT.Exp, act.last())
        p.meet(self.pending(), banks + m_free)
        mbank.append(p.b[2])
        m_free.append(None)
        advance(0)
        self.restack(1)
        self.marks(1)
        N = len(steps)
        for n in range(N + 3):
            wide = 512 - offset(min(n, N - 1))
            before = 512 - offset(min(max(n - 1, 0), N - 1))
            if n < N:
                hg, qt, kt = steps[n]
                while (hg, qt) not in biased:
                    next(gen)
                for j in range(4):
                    score(n, j)
                    advance(wide)
            if 1 <= n <= N:
                weigh(n - 1)
                advance(4 * before)
            if n >= 3 and n % 2:
                total(n - 2)
                advance(4 * before)
            if n < N:
                if steps[n] == (2, 1, 0):
                    out.weight(*[t for j in range(4) for t in self.stacked[(3, j)]])
                if steps[n] == (2, 3, 0):
                    parts.extend(lambda c=c: out.convert(c) for c in range(KC))
                if steps[n] == (3, 2, 2):
                    parts.extend(lambda c=c, q=qt - 2: out.split(q, c, normed[(c, q)], self.last_use[2])
                                 for c in range(KC))
            if n < N and kt == 15 and hg + 2 < 4:
                self.restack(hg + 2)
        for f in parts:
            f()
        return normed, m_free + st_free + av_free + rs_free


class Out:

    def __init__(self, p, b):
        self.p, self.b = p, b
        o = QS0 + 32768
        self.wraw = p.at([128, KC, D], F32, C0 + 8192)
        self.wh, self.wl = (p.at([128, KC, D], F32R, C0 + 16384 + 8192 * i) for i in range(2))
        self.ah = [p.at([128, KC, 512], F32R, x) for x in (KP0, o)]
        self.al = [p.at([128, KC, 512], F32R, x + 8192) for x in (KP0, o)]
        self.xr = [p.at([128, 512], F32, (o + 32768 if i < 12 or b == 0 else XR0 - 24576) + 2048 * i)
                   for i in range(16)]
        self.avn = p.qs[:, :, :, :].rearrange("p g a s -> p g (a s)").bitcast(F32)
        self.kw, self.ka = {}, {}

    def weight(self, *toks):
        p = self.p
        self.kraw = p.dma.go(self.wraw[:, :, :], p.a["L0_attn_Wo"].rearrange("(c p) n -> p c n", p=128), *toks)

    def convert(self, c):
        p = self.p
        k = p.af(self.wh[:, c, :], self.wraw[:, c, :], ACT.Copy, self.kraw)
        self.kw[c] = p.tt(p.dve, self.wl[:, c, :], self.wraw[:, c, :], self.wh[:, c, :], ALU.subtract, k)

    def split(self, q, c, *toks):
        p, i = self.p, q % 2
        x = self.avn[:, c, 512 * q:512 * q + 512]
        k = p.af(self.ah[i][:, c, :], x, ACT.Copy, *toks)
        self.ka[(q, c)] = p.tt(p.dve, self.al[i][:, c, :], x, self.ah[i][:, c, :], ALU.subtract, k)

    def run(self, normed, ring_free, prefetch):
        p, b = self.p, self.b
        dve, pool = p.dve, p.pool
        xr, wh, wl, ah, al = self.xr, self.wh, self.wl, self.ah, self.al
        src = p.xa[S * b:S * (b + 1), :].rearrange("(n t p) d -> n t p d", t=4, p=128)
        dst = p.xc[S * b:S * (b + 1), :].rearrange("(n t p) d -> n t p d", t=4, p=128)
        a_free, done = [None] * 2, []
        beside = prefetch()
        kx = [p.dma.go(xr[n][:, :], src[n // 4, n % 4], p.xa_done[16 * b + n]) for n in range(16)]
        for n in range(16):
            q, tb = divmod(n, 4)
            i, r = q % 2, n % 8
            if tb == 0 and q < 3:
                for c in range(KC):
                    self.split(q + 1, c, normed[(c, q + 1)], a_free[(q + 1) % 2])
            c0 = slice(128 * tb, 128 * tb + 128)
            kb = p.tt(pool, xr[n][:, :], xr[n][:, :], p.bob[:, :], ALU.add, kx[n])
            for c in range(KC):
                p.mm(p.b[r], ah[i][:, c, c0], wh[:, c, :], c == 0, False, ring_free[r], self.ka[(q, c)], self.kw[c])
                p.mm(p.b[r], ah[i][:, c, c0], wl[:, c, :], False, False)
                k = p.mm(p.b[r], al[i][:, c, c0], wh[:, c, :], False, c == KC - 1, sig=c == KC - 1)
            a_free[i] = k
            ring_free[r] = p.tt(dve, xr[n][:, :], p.b[r], xr[n][:, :], ALU.add, k, kb)
            p.xc_done[16 * b + n] = p.dma.go(dst[q, tb], xr[n][:, :], ring_free[r])
            done.append(p.xc_done[16 * b + n])
            if n == 12:
                self.half_free = a_free[0]
            for _ in range(5 if n > 2 else 0):
                next(beside, None)
        for _ in beside:
            pass
        return ring_free, done


def program(nc, a):
    p = Prog(nc, a)
    p.xa = nc.dram_tensor("xa", [T, D], F32).ap()
    p.xc = nc.dram_tensor("xc", [T, D], F32).ap()
    p.xa_done, p.xc_done, out_done = {}, {}, {}
    p.dg = nc.dram_tensor("dg", [IC, 128, 1024], F32).ap()
    p.dd = nc.dram_tensor("dd", [IC, 128, 2 * D], F32).ap()
    p.dk = nc.dram_tensor("dk", [32, 4 * S], F16).ap()
    psum(p)
    constants(p)
    ffn_memory(p)
    p.qs = p.at([128, 4, 2, S], F16, QS0)
    p.ks = p.at([128, 4, 2, S], F16, C0)
    p.v = p.at([128, 16, D], F32, C0 + 32768)
    pieces = weight_pieces(p)
    qkv = [Qkv(p, 0, (A0 + 24576, A0 + 32768, XR0)), Qkv(p, 1, (C0 + 8192, C0, XR0))]

    def prefetched(b):
        return list(qkv[b].kraw.values()) + x_loads[b]

    x_loads = {}

    def ahead_of_qkv(b, free, *toks):
        qkv[b].s_free = [free, None]
        qkv[b].load(0, *toks)
        x_loads[b] = list(qkv[b].kx[0])
        return ahead_steps(b, *toks)

    def ahead_steps(b, *toks):
        for n in (1, 0) if b == 0 else (1, 0, 2):
            qkv[b].weight(n, *toks)
        yield from qkv[b].norm(0)

    x_out, banks = ffn(p, a["L0_attn_X"].rearrange("b s d -> (b s) d"), p.xa, {}, p.xa_done, dequantize=True,
                       ahead=lambda free, *toks: ahead_of_qkv(0, free, *toks))
    qkv[0].weight(2, *x_out)
    p.meet(prefetched(0) + x_out, banks)
    tiles, rest = {}, []
    for b in range(B):
        att, rest_of_qkv, banks = qkv[b].run(x_out if b else [])
        out = Out(p, b)
        normed, banks = att.run(out, rest_of_qkv, banks)
        p.meet([], [])
        if b == 0:
            banks, x_out = out.run(normed, banks, lambda: ahead_of_qkv(1, None))
            p.meet(prefetched(1) + x_out, banks)
        else:
            start = {}

            def ahead_of_ffn():
                start["kn"] = kn = []
                start["kx"] = [p.dma.go(p.xb[tb][:, :], p.xc[128 * tb:128 * tb + 128, :], p.xc_done[tb])
                               for tb in range(4)]
                return fetch(kn)

            def fetch(kn):
                normed_x = norm_steps(p, p.xb, start["kx"], kn, (p.st, p.mv, p.rs, p.w4), None)
                first = [x for i in (0, 1, 2, 3, 4, 8, 9, 10) for x in ((i, 0), (i, 1))
                         if x not in ((4, 0), (8, 1))]
                second = [(i, 1) for i in range(5, 9)]
                for n in range(64):
                    next(normed_x, 0)
                    if n % 3 == 0 and first:
                        x = first.pop(0)
                        tiles[x] = p.dma.go(*pieces[x[0]][x[1]])
                    yield
                for x in first:
                    tiles[x] = p.dma.go(*pieces[x[0]][x[1]])
                for x in second:
                    tiles[x] = p.dma.go(*pieces[x[0]][x[1]], out.half_free)

            banks, x_out = out.run(normed, banks, ahead_of_ffn)
            p.meet(list(tiles.values()) + x_out, banks)
            for i in range(4, 8):
                s, d = pieces[i][0]
                tiles[(i, 0)] = p.dma.go(s, d)
    kg, kd = ({i: [tiles[(i, m)]] for i in range(IC)} for m in range(2))
    ffn(p, p.xc, a["out"].rearrange("b s d -> (b s) d"), p.xc_done, out_done, loaded=(kg, kd), start=start,
        settle=x_out)
    p.meet([], None)
    with nc.Block() as block:
        @block.sync
        def _(e):
            p.sp.run(e)

        @block.tensor
        def _(e):
            p.pe.run(e)

        @block.vector
        def _(e):
            p.dve.run(e)

        @block.scalar
        def _(e):
            p.act.run(e)

        @block.gpsimd
        def _(e):
            p.pool.run(e)


_INS = ["L0_attn_X", "L0_attn_ln_g", "L0_attn_ln_b", "L0_attn_Wq", "L0_attn_bq", "L0_attn_Wk", "L0_attn_bk",
        "L0_attn_Wv", "L0_attn_bv", "L0_attn_Wo", "L0_attn_bo", "L0_ffn_gate_up_packed", "L0_ffn_gate_up_scales",
        "L0_ffn_down_packed", "L0_ffn_down_scales"]


def kernel(**inputs):
    import numpy as np
    import concourse.bacc as bacc
    from concourse.bass_utils import run_bass_kernel_spmd

    nc = bacc.Bacc("TRN2", target_bir_lowering=False, num_devices=1)
    arrays, a = {}, {}
    for name in _INS:
        x = np.ascontiguousarray(inputs[name])
        arrays[name] = x
        a[name] = nc.dram_tensor(name, x.shape, mybir.dt.from_np(x.dtype), kind="ExternalInput").ap()
    a["out"] = nc.dram_tensor("out", (B, S, D), F32, kind="ExternalOutput").ap()
    program(nc, a)
    r = run_bass_kernel_spmd(nc, [arrays], core_ids=[0])
    return r.results[0]["out"]
```
